# Optimizing a Trainium2 kernel written in Bass

```python
import numpy as np
import jax
import jax.numpy as jnp

def _softmax(x, axis=-1):
    return jax.nn.softmax(x, axis=axis)

def _gelu(x):
    return jax.nn.gelu(x, approximate=True)

def _silu(x):
    return jax.nn.silu(x)

def _sigmoid(x):
    return jax.nn.sigmoid(x)

def _layernorm(x, axis=-1, eps=1e-05):
    m = jnp.mean(x, axis=axis, keepdims=True)
    v = jnp.var(x, axis=axis, keepdims=True)
    return (x - m) / jnp.sqrt(v + eps)

def _scatter_add(tgt, idx, src, axis=0):
    return tgt.at[idx].add(src)

def _segment_sum(src, seg, n):
    return jax.ops.segment_sum(src, seg, n)
kernel_name = 'mk_adj_preln_d4_adj_r2_acacd2'

def setup_inputs(seed: int=0):
    np.random.seed(seed)
    _w = jnp.asarray

    def _rec_inputs():
        import jax
        import jax.numpy as jnp
        _gk = jax.random.key(seed)
        x = -0.000929 + 1 * jax.random.normal(jax.random.fold_in(_gk, 1), (128, 128, 256), jnp.float32)
        _a = jax.random.bernoulli(jax.random.fold_in(_gk, 2), 0.03125, (128, 128))
        _a = jnp.logical_or(_a, jnp.swapaxes(_a, -1, -2))
        _a = jnp.logical_or(_a, jnp.eye(128, dtype=bool))
        adj = _a.astype(jnp.int32)
        return (x, adj)
    x, adj = _rec_inputs()

    def _L0_gnn_setup():
        import jax, jax.numpy as jnp
        import numpy as np
        B, K, DIN, DOUT = (32, 64, 256, 256)
        key = jax.random.key(seed)
        k1, k2, k3, k4 = jax.random.split(key, 4)
        x = jax.random.normal(k1, (B, K, DIN), dtype=jnp.float32)
        adj = jax.random.randint(k2, (K, K), 0, 2, dtype=jnp.int32)
        W = jax.random.normal(k3, (DOUT, 2 * DIN), dtype=jnp.float32) * 0.02
        b = jax.random.normal(k4, (DOUT,), dtype=jnp.float32) * 0.02
        return {'x': x, 'adj': adj, 'W': W, 'b': b}
    _L0_gnn_all = _L0_gnn_setup()
    _L0_gnn_in = {k: v for k, v in _L0_gnn_all.items() if k in ('W', 'b')}
    del _L0_gnn_all

    def _L1_gnn_setup():
        import jax, jax.numpy as jnp
        import numpy as np
        B, N, D = (8, 1024, 256)
        NEG_SLOPE = 0.2
        key = jax.random.key(seed)
        k1, k2, k3, k4, k5 = jax.random.split(key, 5)
        x = jax.random.normal(k1, (B, N, D), dtype=jnp.float32)
        adj = jax.random.randint(k2, (N, N), 0, 2, dtype=jnp.int32)
        adj = jnp.maximum(adj, jnp.eye(N, dtype=jnp.int32))
        W = jax.random.normal(k3, (D, D), dtype=jnp.float32) * (1.0 / np.sqrt(D))
        a_src = jax.random.normal(k4, (D,), dtype=jnp.float32) * (1.0 / np.sqrt(D))
        a_dst = jax.random.normal(k5, (D,), dtype=jnp.float32) * (1.0 / np.sqrt(D))
        return {'x': x, 'adj': adj, 'W': W, 'a_src': a_src, 'a_dst': a_dst}
    _L1_gnn_all = _L1_gnn_setup()
    _L1_gnn_in = {k: v for k, v in _L1_gnn_all.items() if k in ('W', 'a_src', 'a_dst')}
    del _L1_gnn_all

    def _L2_gnn_setup():
        import jax, jax.numpy as jnp
        import numpy as np
        B, N, F, F1 = (512, 75, 256, 128)
        NEG = -1000000000.0
        ALPHA = 0.2
        key = jax.random.key(seed)
        k1, k2, k3, k4 = jax.random.split(key, 4)
        X = jax.random.normal(k1, (B, N, F), dtype=jnp.float32)
        A = jax.random.randint(k2, (N, N), 0, 2, dtype=jnp.int32)
        W = jax.random.normal(k3, (F, F1), dtype=jnp.float32) * (1.0 / np.sqrt(F))
        a = jax.random.normal(k4, (2, F1, 1), dtype=jnp.float32) * (1.0 / np.sqrt(F1))
        return {'X': X, 'A': A, 'W': W, 'a': a}
    _L2_gnn_all = _L2_gnn_setup()
    _L2_gnn_in = {k: v for k, v in _L2_gnn_all.items() if k in ('W', 'a')}
    del _L2_gnn_all

    def _L3_gnn_setup():
        import jax, jax.numpy as jnp
        import numpy as np
        D_MODEL = 256
        NUM_HEADS = 8
        D_HEAD = D_MODEL // NUM_HEADS
        B, N = (4, 1024)
        key = jax.random.key(seed)
        ks = jax.random.split(key, 10)
        s = 1.0 / np.sqrt(D_MODEL)
        inp = {'h': jax.random.normal(ks[0], (B, N, D_MODEL), dtype=jnp.float32), 'adj': jax.random.randint(ks[1], (N, N), 0, 2, dtype=jnp.int32), 'Wq': jax.random.uniform(ks[2], (D_MODEL, D_MODEL), jnp.float32, -s, s), 'bq': jax.random.uniform(ks[3], (D_MODEL,), jnp.float32, -s, s), 'Wk': jax.random.uniform(ks[4], (D_MODEL, D_MODEL), jnp.float32, -s, s), 'bk': jax.random.uniform(ks[5], (D_MODEL,), jnp.float32, -s, s), 'Wv': jax.random.uniform(ks[6], (D_MODEL, D_MODEL), jnp.float32, -s, s), 'bv': jax.random.uniform(ks[7], (D_MODEL,), jnp.float32, -s, s), 'Wo': jax.random.uniform(ks[8], (D_MODEL, D_MODEL), jnp.float32, -s, s), 'bo': jax.random.uniform(ks[9], (D_MODEL,), jnp.float32, -s, s)}
        return inp
    _L3_gnn_all = _L3_gnn_setup()
    _L3_gnn_in = {k: v for k, v in _L3_gnn_all.items() if k in ('Wq', 'bq', 'Wk', 'bk', 'Wv', 'bv', 'Wo', 'bo')}
    del _L3_gnn_all
    return {'x': x, 'adj': adj, 'L0_gnn_W': _L0_gnn_in['W'], 'L0_gnn_b': _L0_gnn_in['b'], 'L1_gnn_W': _L1_gnn_in['W'], 'L1_gnn_a_src': _L1_gnn_in['a_src'], 'L1_gnn_a_dst': _L1_gnn_in['a_dst'], 'L2_gnn_W': _L2_gnn_in['W'], 'L2_gnn_a': _L2_gnn_in['a'], 'L3_gnn_Wq': _L3_gnn_in['Wq'], 'L3_gnn_bq': _L3_gnn_in['bq'], 'L3_gnn_Wk': _L3_gnn_in['Wk'], 'L3_gnn_bk': _L3_gnn_in['bk'], 'L3_gnn_Wv': _L3_gnn_in['Wv'], 'L3_gnn_bv': _L3_gnn_in['bv'], 'L3_gnn_Wo': _L3_gnn_in['Wo'], 'L3_gnn_bo': _L3_gnn_in['bo']}

def reference(x, adj, L0_gnn_W, L0_gnn_b, L1_gnn_W, L1_gnn_a_src, L1_gnn_a_dst, L2_gnn_W, L2_gnn_a, L3_gnn_Wq, L3_gnn_bq, L3_gnn_Wk, L3_gnn_bk, L3_gnn_Wv, L3_gnn_bv, L3_gnn_Wo, L3_gnn_bo):
    import jax
    import jax.numpy as jnp

    def _L0_gnn_ref(x, adj, W, b):
        import jax, jax.numpy as jnp
        import numpy as np
        B, K, DIN, DOUT = (32, 64, 256, 256)
        Din = x.shape[-1]
        Wi, Wj = (W[:, :Din], W[:, Din:])
        mi = jnp.einsum('bkd,od->bko', x, Wi)
        mj = jnp.einsum('bkd,od->bko', x, Wj)
        a = adj.astype(x.dtype)
        deg = a.sum(axis=1)
        out = deg[None, :, None] * (mi + b) + jnp.einsum('ij,bjo->bio', a, mj)
        return out

    def _L1_gnn_ref(x, adj, W, a_src, a_dst):
        import jax, jax.numpy as jnp
        import numpy as np
        B, N, D = (8, 1024, 256)
        NEG_SLOPE = 0.2
        Wh = jnp.einsum('bnd,de->bne', x, W)
        e_src = jnp.einsum('bnd,d->bn', Wh, a_src)
        e_dst = jnp.einsum('bnd,d->bn', Wh, a_dst)
        logits = e_src[:, :, None] + e_dst[:, None, :]
        logits = jnp.where(logits >= 0, logits, NEG_SLOPE * logits)
        mask = (adj == 0)[None, :, :]
        logits = jnp.where(mask, -jnp.inf, logits)
        attn = jax.nn.softmax(logits, axis=-1)
        attn = jnp.nan_to_num(attn, nan=0.0)
        out = jnp.einsum('bnm,bmd->bnd', attn, Wh)
        return out

    def _L2_gnn_ref(X, A, W, a):
        import jax, jax.numpy as jnp
        import numpy as np
        B, N, F, F1 = (512, 75, 256, 128)
        NEG = -1000000000.0
        ALPHA = 0.2
        h = jnp.einsum('bnf,fo->bno', X, W)
        att_self = jnp.einsum('bno,od->bnd', h, a[0])
        att_neigh = jnp.einsum('bno,od->bnd', h, a[1])
        e = att_self + jnp.swapaxes(att_neigh, 1, 2)
        e = jax.nn.leaky_relu(e, ALPHA)
        adj = A.astype(h.dtype)
        e = e + NEG * (1.0 - adj)[None, :, :]
        alpha = jax.nn.softmax(e, axis=-1)
        out = jnp.einsum('bij,bjo->bio', alpha, h)
        return jnp.concatenate([out, h], axis=-1)

    def _L3_gnn_ref(h, adj, Wq, bq, Wk, bk, Wv, bv, Wo, bo):
        import jax, jax.numpy as jnp
        import numpy as np
        D_MODEL = 256
        NUM_HEADS = 8
        D_HEAD = D_MODEL // NUM_HEADS
        B, N = (4, 1024)
        b, n, _ = h.shape

        def split_heads(x):
            return x.reshape(b, n, NUM_HEADS, D_HEAD).transpose(0, 2, 1, 3)
        q = split_heads(h @ Wq.T + bq)
        k = split_heads(h @ Wk.T + bk)
        v = split_heads(h @ Wv.T + bv)
        scale = 1.0 / np.sqrt(D_HEAD)
        scores = jnp.einsum('bhqd,bhkd->bhqk', q, k) * scale
        mask = (adj == 0)[None, None, :, :]
        scores = jnp.where(mask, -jnp.inf, scores)
        attn = jax.nn.softmax(scores, axis=-1)
        out = jnp.einsum('bhqk,bhkd->bhqd', attn, v)
        out = out.transpose(0, 2, 1, 3).reshape(b, n, D_MODEL)
        return out @ Wo.T + bo
    h = jnp.maximum(_layernorm(x, axis=-1), 0.0)
    x = x + _L0_gnn_ref(h, adj, L0_gnn_W, L0_gnn_b)
    h = jnp.maximum(_layernorm(x, axis=-1), 0.0)
    x = x + _L1_gnn_ref(h, adj, L1_gnn_W, L1_gnn_a_src, L1_gnn_a_dst)
    h = jnp.maximum(_layernorm(x, axis=-1), 0.0)
    x = x + _L2_gnn_ref(h, adj, L2_gnn_W, L2_gnn_a)
    h = jnp.maximum(_layernorm(x, axis=-1), 0.0)
    x = x + _L3_gnn_ref(h, adj, L3_gnn_Wq, L3_gnn_bq, L3_gnn_Wk, L3_gnn_bk, L3_gnn_Wv, L3_gnn_bv, L3_gnn_Wo, L3_gnn_bo)
    return x

_drawn_inputs = setup_inputs


def setup_inputs(seed=0):
    import zlib

    import numpy as np

    out = dict(_drawn_inputs(seed))
    spreads = {}
    factors = {'L1_gnn_a_src': 34.596,
     'L2_gnn_a': 4.127,
     'L3_gnn_Wq': 8.0,
     'L3_gnn_bq': 58.267,
     'L3_gnn_Wk': 8.0,
     'L3_gnn_bk': 64.0,
     'L3_gnn_bv': 7.877,
     'L3_gnn_bo': 4.245}
    for name, (base, spread) in spreads.items():
        noise = np.random.default_rng([zlib.crc32(name.encode()), seed]).standard_normal(out[name].shape)
        drawn = base * np.exp(spread * noise) if base else spread * noise
        out[name] = jnp.asarray(drawn.astype(out[name].dtype))
    for name, factor in factors.items():
        out[name] = (out[name] * factor).astype(out[name].dtype)
    return out
```

```python
from contextlib import ExitStack

import concourse.bass as bass
from concourse import mybir

F32 = mybir.dt.float32
I32 = mybir.dt.int32
ALU = mybir.AluOpType
ACT = mybir.ActivationFunctionType
AX = mybir.AxisListType

P = 128
D = 256
DC = D // P
G = 2
F1 = 128
HEADS = 8
DH = D // HEADS
HPC = P // DH
NH = G * HEADS
LN_EPS = 1e-5
SLOPE = 0.2
MASKED = -1e30
NEG = 1e9

FIRST_LOOPED = 6
LAG = {"load": -1, "l0": 0, "l1": 1, "l2": 2, "l3": 3, "l3b": 4}

BANK_TASKS = ["u0_done", "u1_done", "pt0_done", "pt1_done", "h1t_done", "pt2_done", "pt3_done", "h2t_done",
              "ot_done", "wh0_done", "wh1_done", "h3t_done", "hh_done", "x4_done", "d1_done", "qt_done",
              "d2_done", "kt_done", "v_done", "at1_done", "x1_done", "at2_done", "x2_done", "x3_done"]
TASK_LAG = {"u0_done": 0, "u1_done": 0, "x1_done": 0,
            "h1t_done": 1, "wh0_done": 1, "wh1_done": 1, "d1_done": 1, "at1_done": 1, "x2_done": 1,
            "h2t_done": 2, "hh_done": 2, "d2_done": 2, "at2_done": 2, "x3_done": 2,
            "h3t_done": 3, "qt_done": 3, "kt_done": 3, "v_done": 3,
            "pt0_done": 4, "pt1_done": 4, "pt2_done": 4, "pt3_done": 4, "ot_done": 4, "x4_done": 4}
NBANKS = 4
assert len(BANK_TASKS) % NBANKS == 0


class Looped:

    def __init__(self, t, offset):
        self.t, self.offset = t, offset


def gnn_kernel(nc, x, adj, w0t, b0, w1, w1t, a1, w2, w2t, a2, wqt, bq, wkt, bk, wvt, bv, wot, bo, out):
    NP = x.shape[0] // G
    last_looped = FIRST_LOOPED + (NP - 2 - FIRST_LOOPED) // 2 * 2
    last_step = NP + LAG["l3b"]

    x_pairs = x.rearrange("(p g) n d -> p n g d", g=G)
    out_pairs = out.rearrange("(p g) n d -> p n g d", g=G)

    with ExitStack() as ctx:
        def sb(name, shape, dt=F32):
            return ctx.enter_context(nc.sbuf_tensor(name, shape, dt))

        def sem(name):
            return ctx.enter_context(nc.semaphore(name))

        adj_i = sb("adj_i", [P, P], I32)
        adj_f = sb("adj_f", [P, P])
        ident = sb("ident", [P, P])
        deg = sb("deg", [P, 1])
        aggr = sb("aggr", [P, 2 * P])
        mask = sb("mask", [P, P])
        mask2 = sb("mask2", [P, P])
        has_any = sb("has_any", [P, 1])
        nan_row = sb("nan_row", [P, 1])
        eps = sb("eps", [P, G])
        minus_one = sb("minus_one", [P, G])
        half = sb("half", [P, G])
        w0_sb = sb("w0_sb", [P, 2 * DC, D])
        w1_sb = sb("w1_sb", [P, DC, D + 2])
        w1t_sb = sb("w1t_sb", [P, DC, D])
        a1_sb = sb("a1_sb", [P, DC, 2])
        w2_sb = sb("w2_sb", [P, DC, F1 + 2])
        w2t_sb = sb("w2t_sb", [P, D])
        a2_sb = sb("a2_sb", [P, 2])
        wq_sb = sb("wq_sb", [P, DC, D])
        wk_sb = sb("wk_sb", [P, DC, D])
        wv_sb = sb("wv_sb", [P, DC, D])
        wo_sb = sb("wo_sb", [P, DC, D])
        bq_sb = sb("bq_sb", [P, DC])
        bk_sb = sb("bk_sb", [P, DC])
        bv_sb = sb("bv_sb", [P, DC])
        deg_b = sb("deg_b", [P, D])
        c3 = sb("c3", [P, D])

        x0 = sb("x0", [P, 2, G, D])
        r0 = sb("r0", [P, 2, G, D])
        h0 = sb("h0", [P, 2, G, D])
        ut = sb("ut", [P, 2, G, DC, 2 * P])
        x1 = sb("x1", [P, 2, G, D])
        x2 = sb("x2", [P, 2, G, D])
        x3 = sb("x3", [P, 2, G, D])
        r3 = sb("r3", [P, 2, G, D])
        x4 = sb("x4", [P, 2, G, D])
        y = [None] + [sb(f"y{i}", [P, 2, G, D]) for i in (1, 2, 3)]
        ht = [None] + [sb(f"ht{i}", [P, 2, DC, G, P]) for i in (1, 2, 3)]
        wh = sb("wh", [P, 2, G, D + 2])
        hh = sb("hh", [P, 2, G, F1 + 2])
        z = [None] + [sb(f"z{i}", [P, 2, G, P]) for i in (1, 2)]
        ez = [None] + [sb(f"ez{i}", [P, 2, G, P]) for i in (1, 2)]
        at = [None] + [sb(f"at{i}", [P, 2, G, P]) for i in (1, 2)]
        stats = [sb(f"stats{i}", [P, 2, G, 6]) for i in range(4)]
        mv = [sb(f"mv{i}", [P, 2, G, 2]) for i in range(4)]
        rstd = [sb(f"rstd{i}", [P, 2, G]) for i in range(4)]
        veps = [sb(f"veps{i}", [P, 2, G]) for i in range(4)]
        negmean = sb("negmean", [P, 2, G])
        nmr = sb("nmr", [P, 2, G])
        nmax = [None] + [sb(f"nmax{i}", [P, 2, G]) for i in (1, 2)]
        ssum = [None] + [sb(f"ssum{i}", [P, 2, G]) for i in (1, 2)]
        rsum = [None] + [sb(f"rsum{i}", [P, 2, G]) for i in (1, 2)]
        qt = sb("qt", [P, 2, DC, G * P])
        kt = sb("kt", [P, 2, DC, G * P])
        v = sb("v", [P, 2, G, D])
        s3 = sb("s3", [P, HPC, DC * G, P])
        e3 = sb("e3", [P, HPC, DC * G, P])
        p3 = sb("p3", [P, HPC, DC * G, P])
        pt = sb("pt", [P, HPC, DC * G, P])
        nmax3 = sb("nmax3", [P, 2, HPC, DC * G])
        ssum3 = sb("ssum3", [P, 2, HPC, DC * G])
        rsum3 = sb("rsum3", [P, 2, HPC, DC * G])
        ot = sb("ot", [P, 2, DC, G * P])

        score_bank = [ctx.enter_context(nc.psum_tensor(f"score_bank{i}", [P, 512], F32)) for i in range(HPC)]
        general_bank = [ctx.enter_context(nc.psum_tensor(f"general_bank{i}", [P, 512], F32)) for i in range(NBANKS)]

        def bank_of(task):
            return general_bank[BANK_TASKS.index(task) % NBANKS]

        weights_in, adj_in = sem("weights_in"), sem("adj_in")
        c_pool, c_dve, c_pe = sem("c_pool"), sem("c_dve"), sem("c_pe")
        x_in = [sem("x_in_even"), sem("x_in_odd")]
        x_out = [sem("x_out_even"), sem("x_out_odd")]
        S = {}
        for name in BANK_TASKS:
            S[name] = sem(name)
        for name in ("u0_full", "u1_full", "x1_full", "h1t_full", "wh0_full", "wh1_full", "d1_full", "at1_full",
                     "x2_full", "h2t_full", "hh_full", "d2_full", "at2_full", "x3_full", "h3t_full", "qt_full",
                     "kt_full", "v_full", "pt0_full", "pt1_full", "pt2_full", "pt3_full", "ot_full", "x4_full",
                     "scores_full"):
            S[name] = sem(name)
        for i in range(4):
            S[f"stats{i}"] = sem(f"stats{i}")
            S[f"mv{i}"] = sem(f"mv{i}")
            S[f"veps{i}"] = sem(f"veps{i}")
            S[f"rstd{i}"] = sem(f"rstd{i}")
            if i:
                S[f"y{i}"] = sem(f"y{i}")
        for i in (1, 2):
            for name in ("lin", "leaky", "logit", "nmax", "exp", "rsum"):
                S[f"{name}{i}"] = sem(f"{name}{i}")
        for name in ("negmean", "nmr", "h0", "r0", "r3", "x3_tail", "scores_masked", "nmax3", "exp3", "rsum3", "p3_0", "p3_1", "p3_2", "p3_3", "rany1"):
            S[name] = sem(name)

        at_offset = {}

        def pair(t, k, stage):
            lag = LAG[stage]
            if isinstance(t, int) and not 0 <= t + k - lag < NP:
                return None, 0
            return (k - lag if isinstance(t, int) and t == 0 else Looped(t, k - lag)), (k - lag) % 2

        def passed(eng, name, p, back=0):
            if isinstance(p, Looped):
                eng.wait_ge(S[name], at_offset[p.offset + 1 - back])
            elif p - back >= 0:
                eng.wait_ge(S[name], p + 1 - back)

        def dma_count(p, b, back=0):
            return ((p - back) // 2 + 1) * 16 if isinstance(p, int) else (p.t + (p.offset + 2 - b - back)) * 8

        def index(p):
            return p if isinstance(p, int) else p.t + p.offset

        def bank_free(pe, task, t, k):
            i, back = BANK_TASKS.index(task) - NBANKS, 0
            while True:
                if i < 0:
                    i, back = i + len(BANK_TASKS), back + 1
                before = BANK_TASKS[i]
                lag = TASK_LAG[before]
                if not isinstance(t, int):
                    pe.wait_ge(S[before], at_offset[k - back - lag + 1])
                    return
                if t + k - back < 0:
                    return
                if 0 <= t + k - back - lag < NP:
                    pe.wait_ge(S[before], t + k - back - lag + 1)
                    return
                i -= NBANKS

        def run_steps(eng, step):
            for s in range(FIRST_LOOPED):
                step(0, s)
            with eng.Fori(FIRST_LOOPED, last_looped, 2) as t:
                at_offset.clear()
                for offset in range(-FIRST_LOOPED + 1, 3):
                    at_offset[offset] = eng.snap(eng.to_reg(t + offset))
                step(t, 0)
                step(t, 1)
            for s in range(last_looped, last_step):
                step(0, s)

        block = ctx.enter_context(nc.Block())

        @block.sync
        def _(sp):
            sp.dma_start(adj_i[:], adj).then_inc(adj_in, 16)

            def load(p, b):
                if not isinstance(p, int) or p >= 2:
                    passed(sp, "h0", p, 2)
                    passed(sp, "r0", p, 2)
                sp.dma_start(x0[:, b], x_pairs[bass.ds(index(p), 1)].rearrange("o n g d -> (o n) g d")).then_inc(x_in[b], 16)

            load(0, 0)
            for dst, src in ((w0_sb[:], w0t.rearrange("(c p) o -> p c o", p=P)),
                             (deg_b[:], b0.partition_broadcast(P)),
                             (w1_sb[:, :, 0:D], w1.rearrange("(c p) o -> p c o", p=P)),
                             (w1t_sb[:], w1t.rearrange("(c p) o -> p c o", p=P)),
                             (a1_sb[:], a1.rearrange("(c p) o -> p c o", p=P)),
                             (w2_sb[:, :, 0:F1], w2.rearrange("(c p) o -> p c o", p=P)),
                             (w2t_sb[:], w2t), (a2_sb[:], a2),
                             (wq_sb[:], wqt.rearrange("(c p) o -> p c o", p=P)),
                             (wk_sb[:], wkt.rearrange("(c p) o -> p c o", p=P)),
                             (wv_sb[:], wvt.rearrange("(c p) o -> p c o", p=P)),
                             (wo_sb[:], wot.rearrange("(c p) o -> p c o", p=P)),
                             (bq_sb[:], bq), (bk_sb[:], bk), (bv_sb[:], bv),
                             (c3[:], bo.partition_broadcast(P))):
                sp.dma_start(dst, src).then_inc(weights_in, 16)

            def step(t, k):
                p, b = pair(t, k, "load")
                if p is not None:
                    load(p, b)
                p, b = pair(t, k, "l3b")
                if p is not None:
                    passed(sp, "x4_done", p)
                    sp.dma_start(out_pairs[bass.ds(index(p), 1)].rearrange("o n g d -> (o n) g d"), x4[:, b]).then_inc(x_out[b], 16)

            run_steps(sp, step)
            sp.wait_ge(x_out[0], 16 * (NP // 2))
            sp.wait_ge(x_out[1], 16 * (NP // 2))

        n_weights = 16

        @block.gpsimd
        def _(pool):
            pool.memset(half[:], -0.5).then_inc(c_pool, 1)
            pool.memset(eps[:], LN_EPS)
            pool.memset(minus_one[:], -1.0)
            pool.memset(ident[:], 0.0).then_inc(c_pool, 1)
            pool.wait_ge(c_pool, 2)
            pool.affine_select(out=ident[:], in_=ident[:], compare_op=ALU.not_equal, fill=1.0, base=0,
                               pattern=[[-1, P]], channel_multiplier=1).then_inc(c_pool, 1)
            pool.wait_ge(c_dve, 8)

            def norm_scale(i, p, b):
                passed(pool, f"mv{i}", p)
                passed(pool, "h0" if i == 0 else f"y{i}", p, 2)
                pool.tensor_tensor(veps[i][:, b], mv[i][:, b, :, 1], eps[:], ALU.add).then_inc(S[f"veps{i}"], 1)
                passed(pool, f"veps{i}", p)
                pool.tensor_tensor(rstd[i][:, b], veps[i][:, b], half[:], ALU.pow).then_inc(S[f"rstd{i}"], 1)

            def normalise_p3(j, p, b):
                passed(pool, f"pt{j}_full", p, 1)
                pool.tensor_tensor(p3[:, j], e3[:, j], rsum3[:, b, j].unsqueeze(2).to_broadcast([P, DC * G, P]),
                                   ALU.mult).then_inc(S[f"p3_{j}"], 1)

            def step(t, k):
                p0, b0_ = pair(t, k, "l0")
                p1, b1 = pair(t, k, "l1")
                p2, b2 = pair(t, k, "l2")
                p3_, b3 = pair(t, k, "l3")
                p4, b4 = pair(t, k, "l3b")
                if p0 is not None:
                    norm_scale(0, p0, b0_)
                    passed(pool, "h0", p0, 2)
                    pool.tensor_tensor(negmean[:, b0_], mv[0][:, b0_, :, 0], minus_one[:], ALU.mult).then_inc(S["negmean"], 1)
                    passed(pool, "negmean", p0)
                    passed(pool, "rstd0", p0)
                    pool.tensor_tensor(nmr[:, b0_], negmean[:, b0_], rstd[0][:, b0_], ALU.mult).then_inc(S["nmr"], 1)
                if p3_ is not None:
                    norm_scale(3, p3_, b3)
                if p4 is not None:
                    passed(pool, "rsum3", p4)
                    passed(pool, "exp3", p4)
                    normalise_p3(0, p4, b4)
                    normalise_p3(1, p4, b4)
                    normalise_p3(2, p4, b4)
                    normalise_p3(3, p4, b4)
                if p0 is not None:
                    pool.wait_ge(x_in[b0_], dma_count(p0, b0_))
                    passed(pool, "x1_done", p0, 2)
                    pool.tensor_tensor(r0[:, b0_], x0[:, b0_], deg_b[:].unsqueeze(1).to_broadcast([P, G, D]),
                                       ALU.add).then_inc(S["r0"], 1)
                if p3_ is not None:
                    passed(pool, "x4_done", p3_, 2)
                    passed(pool, "x3_done", p3_)
                    pool.tensor_tensor(r3[:, b3], x3[:, b3], c3[:].unsqueeze(1).to_broadcast([P, G, D]),
                                       ALU.add).then_inc(S["r3"], 1)
                if p2 is not None:
                    passed(pool, "hh_done", p2)
                    passed(pool, "y3", p2, 2)
                    passed(pool, "r3", p2, 2)
                    pool.tensor_tensor(x3[:, b2, :, F1:D], x2[:, b2, :, F1:D], hh[:, b2, :, 0:F1],
                                       ALU.add).then_inc(S["x3_tail"], 1)
                if p0 is not None:
                    norm_scale(1, p0, b0_)
                if p1 is not None:
                    norm_scale(2, p1, b1)

            run_steps(pool, step)

        @block.vector
        def _(dve):
            dve.wait_ge(adj_in, 16)
            dve.tensor_copy(adj_f[:], adj_i[:]).then_inc(c_dve, 1)
            dve.wait_ge(c_dve, 1)
            dve.reduce_sum(deg[:], adj_f[:], AX.X).then_inc(c_dve, 1)
            dve.tensor_scalar(mask[:], adj_f[:], 0.0, MASKED, ALU.is_equal, ALU.mult).then_inc(c_dve, 1)
            dve.tensor_scalar(mask2[:], adj_f[:], 1.0, NEG, ALU.subtract, ALU.mult)
            dve.wait_ge(c_dve, 3)
            dve.wait_ge(c_pool, 3)
            dve.tensor_scalar(aggr[:, P:2 * P], ident[:], deg[:], None, ALU.mult)
            dve.wait_ge(weights_in, 16 * n_weights)
            dve.tensor_scalar(deg_b[:], deg_b[:], deg[:], None, ALU.mult)
            dve.reduce_max(has_any[:], mask[:], AX.X).then_inc(c_dve, 1)
            dve.wait_ge(c_dve, 4)
            dve.tensor_scalar(has_any[:], has_any[:], 0.0, None, ALU.is_equal).then_inc(c_dve, 1)
            dve.wait_ge(c_dve, 5)
            dve.reciprocal(nan_row[:], has_any[:]).then_inc(c_dve, 1)
            dve.wait_ge(c_dve, 6)
            dve.tensor_scalar(nan_row[:], nan_row[:], 0.0, None, ALU.mult).then_inc(c_dve, 1)
            dve.wait_ge(c_pe, 1)
            dve.wait_ge(c_dve, 7)
            dve.tensor_copy(aggr[:, 0:P], general_bank[0][:, 0:P])
            for c in range(DC):
                dve.tensor_copy(w1_sb[:, c, D:D + 2], general_bank[1][:, 2 * c:2 * c + 2])
                dve.tensor_copy(w2_sb[:, c, F1:F1 + 2], general_bank[2][:, 2 * c:2 * c + 2])
            dve.scalar_tensor_tensor(c3[:], general_bank[3][:, 0:D], nan_row[:], c3[:], ALU.add, ALU.add).then_inc(c_dve, 1)

            def norm_stats(i, src, p, b):
                passed(dve, f"rstd{i}", p, 2)
                if i == 0:
                    passed(dve, "negmean", p, 2)
                passed(dve, "h0" if i == 0 else f"y{i}", p, 2)
                for g in range(G):
                    last = dve.bn_stats(stats[i][:, b, g], src[:, b, g])
                last.then_inc(S[f"stats{i}"], 1)
                dve.wait_ge(c_dve, 8)
                passed(dve, f"stats{i}", p)
                for g in range(G):
                    last = dve.bn_aggr(mv[i][:, b, g], stats[i][:, b, g])
                last.then_inc(S[f"mv{i}"], 1)

            def normalise(i, src, p, b):
                passed(dve, f"rstd{i}", p)
                passed(dve, f"mv{i}", p)
                passed(dve, f"h{i}t_full", p, 2)
                for g in range(G):
                    last = dve.tensor_scalar(y[i][:, b, g], src[:, b, g], mv[i][:, b, g, 0:1], rstd[i][:, b, g:g + 1],
                                             ALU.subtract, ALU.mult)
                last.then_inc(S[f"y{i}"], 1)

            def logits(i, src, scol, msk, p, b):
                passed(dve, f"d{i}_full", p)
                passed(dve, f"exp{i}", p, 2)
                bank = bank_of(f"d{i}_done")
                for g in range(G):
                    last = dve.tensor_scalar(z[i][:, b, g], bank[:, g * P:(g + 1) * P], src[:, b, g, scol:scol + 1], None, ALU.add)
                last.then_inc(S[f"d{i}_done"], 1)
                passed(dve, f"d{i}_done", p)
                dve.scalar_tensor_tensor(z[i][:, b], z[i][:, b], SLOPE, z[i][:, b], ALU.mult, ALU.max).then_inc(S[f"leaky{i}"], 1)
                passed(dve, f"leaky{i}", p)
                dve.tensor_tensor(z[i][:, b], z[i][:, b], msk[:].unsqueeze(1).to_broadcast([P, G, P]), ALU.add).then_inc(S[f"logit{i}"], 1)
                passed(dve, f"logit{i}", p)
                dve.tensor_reduce(nmax[i][:, b], z[i][:, b], AX.X, ALU.max, negate=True).then_inc(S[f"nmax{i}"], 1)

            def step(t, k):
                p, b = pair(t, k, "l0")
                if p is not None:
                    dve.wait_ge(x_in[b], dma_count(p, b))
                    norm_stats(0, x0, p, b)
                p, b = pair(t, k, "l1")
                if p is not None:
                    normalise(1, x1, p, b)
                p, b = pair(t, k, "l3b")
                if p is not None:
                    passed(dve, "exp3", p)
                    passed(dve, "p3_3", p, 2)
                    dve.reciprocal(rsum3[:, b], ssum3[:, b]).then_inc(S["rsum3"], 1)
                p, b = pair(t, k, "l2")
                if p is not None:
                    normalise(2, x2, p, b)
                p, b = pair(t, k, "l3")
                if p is not None:
                    passed(dve, "x3_tail", p)
                    norm_stats(3, x3, p, b)
                    normalise(3, x3, p, b)
                p, b = pair(t, k, "l3b")
                if p is not None:
                    passed(dve, "ot_full", p)
                    passed(dve, "x4_full", p, 2)
                    dve.tensor_copy(ot[:, b].rearrange("p c n -> p (c n)"), bank_of("ot_done")[:]).then_inc(S["ot_done"], 1)
                p, b = pair(t, k, "l1")
                if p is not None:
                    logits(1, wh, D, mask, p, b)
                p4, b4 = pair(t, k, "l3b")
                if p4 is not None:
                    passed(dve, "x4_full", p4)
                    passed(dve, "r3", p4)
                    if not isinstance(p4, int) or p4 >= 2:
                        dve.wait_ge(x_out[b4], dma_count(p4, b4, 2))
                    dve.tensor_tensor(x4[:, b4].rearrange("p g d -> p (g d)"), bank_of("x4_done")[:],
                                      r3[:, b4].rearrange("p g d -> p (g d)"), ALU.add).then_inc(S["x4_done"], 1)
                p3_, b3 = pair(t, k, "l3")
                if p3_ is not None:
                    passed(dve, "qt_full", p3_)
                    passed(dve, "scores_full", p3_, 2)
                    for c in range(DC):
                        last = dve.tensor_scalar(qt[:, b3, c], bank_of("qt_done")[:, c * G * P:(c + 1) * G * P], bq_sb[:, c:c + 1], None, ALU.add)
                    last.then_inc(S["qt_done"], 1)
                p, b = pair(t, k, "l2")
                if p is not None:
                    logits(2, hh, F1, mask2, p, b)
                if p3_ is not None:
                    passed(dve, "kt_full", p3_)
                    for c in range(DC):
                        last = dve.tensor_scalar(kt[:, b3, c], bank_of("kt_done")[:, c * G * P:(c + 1) * G * P], bk_sb[:, c:c + 1], None, ALU.add)
                    last.then_inc(S["kt_done"], 1)
                p, b = pair(t, k, "l1")
                if p is not None:
                    passed(dve, "exp1", p)
                    passed(dve, "x2_done", p, 2)
                    dve.reciprocal(rsum[1][:, b], ssum[1][:, b]).then_inc(S["rany1"], 1)
                    passed(dve, "rany1", p)
                    dve.tensor_scalar(rsum[1][:, b], rsum[1][:, b], has_any[:], None, ALU.mult).then_inc(S["rsum1"], 1)
                    passed(dve, "at1_full", p)
                    passed(dve, "x2_full", p, 2)
                    dve.tensor_copy(at[1][:, b].rearrange("p g n -> p (g n)"), bank_of("at1_done")[:, 0:G * P]).then_inc(S["at1_done"], 1)
                p, b = pair(t, k, "l0")
                if p is not None:
                    passed(dve, "x1_full", p)
                    passed(dve, "r0", p)
                    passed(dve, "x2_done", p, 2)
                    passed(dve, "y1", p, 2)
                    dve.tensor_tensor(x1[:, b].rearrange("p g d -> p (g d)"), bank_of("x1_done")[:],
                                      r0[:, b].rearrange("p g d -> p (g d)"), ALU.add).then_inc(S["x1_done"], 1)
                    passed(dve, "x1_done", p)
                    norm_stats(1, x1, p, b)
                p, b = pair(t, k, "l2")
                if p is not None:
                    passed(dve, "exp2", p)
                    passed(dve, "x3_done", p, 2)
                    dve.reciprocal(rsum[2][:, b], ssum[2][:, b]).then_inc(S["rsum2"], 1)
                    passed(dve, "at2_full", p)
                    passed(dve, "x3_full", p, 2)
                    dve.tensor_copy(at[2][:, b].rearrange("p g n -> p (g n)"), bank_of("at2_done")[:, 0:G * P]).then_inc(S["at2_done"], 1)
                if p3_ is not None:
                    passed(dve, "scores_full", p3_)
                    passed(dve, "exp3", p3_, 1)
                    for j in range(HPC):
                        last = dve.scalar_tensor_tensor(s3[:, j], score_bank[j][:].rearrange("p (b n) -> p b n", n=P), float(DH) ** -0.5,
                                                        mask[:].unsqueeze(1).to_broadcast([P, DC * G, P]), ALU.mult, ALU.add)
                    last.then_inc(S["scores_masked"], 1)
                    passed(dve, "scores_masked", p3_)
                    dve.tensor_reduce(nmax3[:, b3], s3[:], AX.X, ALU.max, negate=True).then_inc(S["nmax3"], 1)
                p, b = pair(t, k, "l1")
                if p is not None:
                    passed(dve, "x2_full", p)
                    passed(dve, "rsum1", p)
                    passed(dve, "x3_done", p, 2)
                    passed(dve, "x3_tail", p, 2)
                    passed(dve, "y2", p, 2)
                    for g in range(G):
                        last = dve.scalar_tensor_tensor(x2[:, b, g], bank_of("x2_done")[:, g * D:(g + 1) * D], rsum[1][:, b, g:g + 1],
                                                        x1[:, b, g], ALU.mult, ALU.add)
                    last.then_inc(S["x2_done"], 1)
                    passed(dve, "x2_done", p)
                    norm_stats(2, x2, p, b)
                p, b = pair(t, k, "l2")
                if p is not None:
                    passed(dve, "x3_full", p)
                    passed(dve, "rsum2", p)
                    passed(dve, "y3", p, 2)
                    passed(dve, "r3", p, 2)
                    for g in range(G):
                        last = dve.scalar_tensor_tensor(x3[:, b, g, 0:F1], bank_of("x3_done")[:, g * F1:(g + 1) * F1], rsum[2][:, b, g:g + 1],
                                                        x2[:, b, g, 0:F1], ALU.mult, ALU.add)
                    last.then_inc(S["x3_done"], 1)
                    passed(dve, "x3_done", p)

            run_steps(dve, step)

        @block.scalar
        def _(act):
            act.wait_ge(weights_in, 16 * n_weights)

            def exps(i, p, b):
                passed(act, f"nmax{i}", p)
                passed(act, f"at{i}_full", p, 2)
                passed(act, f"rsum{i}", p, 2)
                for g in range(G):
                    last = act.activation(ez[i][:, b, g], z[i][:, b, g], ACT.Exp, bias=nmax[i][:, b, g:g + 1],
                                          accum_out=ssum[i][:, b, g:g + 1])
                last.then_inc(S[f"exp{i}"], 1)

            def relu_transposed(i, p, b, reader):
                passed(act, f"h{i}t_full", p)
                passed(act, reader, p, 2)
                act.activation(ht[i][:, b].rearrange("p c g n -> p (c g n)"), bank_of(f"h{i}t_done")[:], ACT.Relu).then_inc(S[f"h{i}t_done"], 1)

            def step(t, k):
                p, b = pair(t, k, "l0")
                if p is not None:
                    passed(act, "rstd0", p)
                    passed(act, "mv0", p)
                    passed(act, "u1_full", p, 2)
                    passed(act, "nmr", p)
                    for g in range(G):
                        last = act.activation(h0[:, b, g], x0[:, b, g], ACT.Relu, bias=nmr[:, b, g:g + 1], scale=rstd[0][:, b, g:g + 1])
                    last.then_inc(S["h0"], 1)
                    for g in range(G):
                        passed(act, f"u{g}_full", p)
                        passed(act, "x1_full", p, 2)
                        act.activation(ut[:, b, g].rearrange("p c n -> p (c n)"), bank_of(f"u{g}_done")[:], ACT.Copy).then_inc(S[f"u{g}_done"], 1)
                p4, b4 = pair(t, k, "l3b")
                if p4 is not None:
                    for j in range(2):
                        passed(act, f"pt{j}_full", p4)
                        passed(act, "ot_full", p4, 1)
                        act.activation(pt[:, j].rearrange("p b n -> p (b n)"), bank_of(f"pt{j}_done")[:], ACT.Copy).then_inc(S[f"pt{j}_done"], 1)
                p, b = pair(t, k, "l1")
                if p is not None:
                    relu_transposed(1, p, b, "wh1_full")
                if p4 is not None:
                    for j in range(2, HPC):
                        passed(act, f"pt{j}_full", p4)
                        act.activation(pt[:, j].rearrange("p b n -> p (b n)"), bank_of(f"pt{j}_done")[:], ACT.Copy).then_inc(S[f"pt{j}_done"], 1)
                p2, b2 = pair(t, k, "l2")
                if p2 is not None:
                    relu_transposed(2, p2, b2, "hh_full")
                if p is not None:
                    for g in range(G):
                        passed(act, f"wh{g}_full", p)
                        passed(act, "x2_full", p, 2)
                        passed(act, "d1_done", p, 2)
                        act.activation(wh[:, b, g], bank_of(f"wh{g}_done")[:, 0:D + 2], ACT.Copy).then_inc(S[f"wh{g}_done"], 1)
                p3_, b3 = pair(t, k, "l3")
                if p3_ is not None:
                    relu_transposed(3, p3_, b3, "v_full")
                if p2 is not None:
                    passed(act, "hh_full", p2)
                    passed(act, "x3_full", p2, 2)
                    passed(act, "d2_done", p2, 2)
                    passed(act, "x3_tail", p2, 2)
                    act.activation(hh[:, b2].rearrange("p g n -> p (g n)"), bank_of("hh_done")[:, 0:G * (F1 + 2)], ACT.Copy).then_inc(S["hh_done"], 1)
                if p is not None:
                    exps(1, p, b)
                if p2 is not None:
                    exps(2, p2, b2)
                if p3_ is not None:
                    passed(act, "v_full", p3_)
                    passed(act, "ot_full", p3_, 2)
                    act.activation(v[:, b3].rearrange("p g d -> p (g d)"), bank_of("v_done")[:], ACT.Copy).then_inc(S["v_done"], 1)
                    passed(act, "nmax3", p3_)
                    passed(act, "rsum3", p3_, 2)
                    for j in range(HPC):
                        passed(act, f"p3_{j}", p3_, 1)
                        for i in range(DC * G):
                            last = act.activation(e3[:, j, i], s3[:, j, i], ACT.Exp, bias=nmax3[:, b3, j, i:i + 1],
                                                  accum_out=ssum3[:, b3, j, i:i + 1])
                    last.then_inc(S["exp3"], 1)

            run_steps(act, step)

        @block.tensor
        def _(pe):
            pe.wait_ge(c_pool, 3)
            pe.wait_ge(c_dve, 1)
            pe.wait_ge(weights_in, 16 * n_weights)
            pe.transpose(general_bank[0][:, 0:P], adj_f[:], ident[:])
            for c in range(DC):
                for e in range(DC):
                    pe.matmul(general_bank[1][:, 2 * c:2 * c + 2], w1t_sb[:, e, c * P:(c + 1) * P], a1_sb[:, e, :],
                              start=(e == 0), stop=(e == DC - 1))
                pe.matmul(general_bank[2][:, 2 * c:2 * c + 2], w2t_sb[:, c * P:(c + 1) * P], a2_sb[:], start=True, stop=True)
            for c in range(DC):
                last = pe.matmul(general_bank[3][:, 0:D], bv_sb[:, c:c + 1].to_broadcast([P, P]), wo_sb[:, c, :],
                                 start=(c == 0), stop=(c == DC - 1))
            last.then_inc(c_pe, 1)
            pe.wait_ge(c_dve, 8)

            def transpose_y(i, p, b, t, k):
                passed(pe, f"y{i}", p)
                bank_free(pe, f"h{i}t_done", t, k)
                for c in range(DC):
                    for g in range(G):
                        last = pe.transpose(bank_of(f"h{i}t_done")[:, (c * G + g) * P:(c * G + g + 1) * P], y[i][:, b, g, c * P:(c + 1) * P], ident[:])
                last.then_inc(S[f"h{i}t_full"], 1)

            def spread_dst(i, src, col, p, b, t, k):
                bank_free(pe, f"d{i}_done", t, k)
                for g in range(G):
                    last = pe.transpose(bank_of(f"d{i}_done")[:, g * P:(g + 1) * P], src[:, b, g, col:col + 1].to_broadcast([P, P]), ident[:])
                last.then_inc(S[f"d{i}_full"], 1)

            def transpose_exp(i, p, b, t, k):
                passed(pe, f"exp{i}", p)
                bank_free(pe, f"at{i}_done", t, k)
                for g in range(G):
                    last = pe.transpose(bank_of(f"at{i}_done")[:, g * P:(g + 1) * P], ez[i][:, b, g], ident[:])
                last.then_inc(S[f"at{i}_full"], 1)

            def transpose_p3(j, p, b, t, k):
                passed(pe, f"p3_{j}", p)
                bank_free(pe, f"pt{j}_done", t, k)
                for i in range(DC * G):
                    last = pe.transpose(bank_of(f"pt{j}_done")[:, i * P:(i + 1) * P], p3[:, j, i], ident[:])
                last.then_inc(S[f"pt{j}_full"], 1)

            def step(t, k):
                p0, b0_ = pair(t, k, "l0")
                p1, b1 = pair(t, k, "l1")
                p2, b2 = pair(t, k, "l2")
                p3_, b3 = pair(t, k, "l3")
                p4, b4 = pair(t, k, "l3b")
                if p0 is not None:
                    passed(pe, "h0", p0)
                    for g in range(G):
                        bank_free(pe, f"u{g}_done", t, k)
                        for c in range(DC):
                            last = pe.matmul(bank_of(f"u{g}_done")[:, c * 2 * P:(c + 1) * 2 * P], h0[:, b0_, g, c * P:(c + 1) * P], aggr[:], start=True, stop=True)
                        last.then_inc(S[f"u{g}_full"], 1)
                if p4 is not None:
                    transpose_p3(0, p4, b4, t, k)
                    transpose_p3(1, p4, b4, t, k)
                if p1 is not None:
                    transpose_y(1, p1, b1, t, k)
                if p4 is not None:
                    transpose_p3(2, p4, b4, t, k)
                    transpose_p3(3, p4, b4, t, k)
                if p2 is not None:
                    transpose_y(2, p2, b2, t, k)
                if p4 is not None:
                    for j in range(HPC):
                        passed(pe, f"pt{j}_done", p4)
                    passed(pe, "v_done", p4)
                    bank_free(pe, "ot_done", t, k)
                    for c in range(DC):
                        for g in range(G):
                            for j in range(HPC):
                                last = pe.matmul(bank_of("ot_done")[j * DH:(j + 1) * DH, (c * G + g) * P:(c * G + g + 1) * P],
                                                 v[:, b4, g, c * P + j * DH:c * P + (j + 1) * DH], pt[:, j, c * G + g], start=True, stop=True, tile_position=(0, j * DH))
                    last.then_inc(S["ot_full"], 1)
                if p1 is not None:
                    passed(pe, "h1t_done", p1)
                    for g in range(G):
                        bank_free(pe, f"wh{g}_done", t, k)
                        for c in range(DC):
                            last = pe.matmul(bank_of(f"wh{g}_done")[:, 0:D + 2], ht[1][:, b1, c, g], w1_sb[:, c, :], start=(c == 0), stop=(c == DC - 1))
                        last.then_inc(S[f"wh{g}_full"], 1)
                if p3_ is not None:
                    transpose_y(3, p3_, b3, t, k)
                if p2 is not None:
                    passed(pe, "h2t_done", p2)
                    bank_free(pe, "hh_done", t, k)
                    for g in range(G):
                        for c in range(DC):
                            last = pe.matmul(bank_of("hh_done")[:, g * (F1 + 2):(g + 1) * (F1 + 2)], ht[2][:, b2, c, g], w2_sb[:, c, :], start=(c == 0), stop=(c == DC - 1))
                    last.then_inc(S["hh_full"], 1)
                if p4 is not None:
                    passed(pe, "ot_done", p4)
                    bank_free(pe, "x4_done", t, k)
                    for g in range(G):
                        for c in range(DC):
                            last = pe.matmul(bank_of("x4_done")[:, g * D:(g + 1) * D], ot[:, b4, c, g * P:(g + 1) * P], wo_sb[:, c, :], start=(c == 0), stop=(c == DC - 1))
                    last.then_inc(S["x4_full"], 1)
                if p1 is not None:
                    passed(pe, "wh0_done", p1)
                    passed(pe, "wh1_done", p1)
                    spread_dst(1, wh, D + 1, p1, b1, t, k)
                if p3_ is not None:
                    passed(pe, "h3t_done", p3_)
                    for name, w in (("qt", wq_sb), ):
                        bank_free(pe, f"{name}_done", t, k)
                        for o in range(DC):
                            for c in range(DC):
                                last = pe.matmul(bank_of(f"{name}_done")[:, o * G * P:(o + 1) * G * P], w[:, c, o * P:(o + 1) * P],
                                                 ht[3][:, b3, c].rearrange("p g n -> p (g n)"), start=(c == 0), stop=(c == DC - 1))
                        last.then_inc(S[f"{name}_full"], 1)
                if p2 is not None:
                    passed(pe, "hh_done", p2)
                    spread_dst(2, hh, F1 + 1, p2, b2, t, k)
                if p3_ is not None:
                    bank_free(pe, "kt_done", t, k)
                    for o in range(DC):
                        for c in range(DC):
                            last = pe.matmul(bank_of("kt_done")[:, o * G * P:(o + 1) * G * P], wk_sb[:, c, o * P:(o + 1) * P],
                                             ht[3][:, b3, c].rearrange("p g n -> p (g n)"), start=(c == 0), stop=(c == DC - 1))
                    last.then_inc(S["kt_full"], 1)
                    bank_free(pe, "v_done", t, k)
                    for g in range(G):
                        for c in range(DC):
                            last = pe.matmul(bank_of("v_done")[:, g * D:(g + 1) * D], ht[3][:, b3, c, g], wv_sb[:, c, :], start=(c == 0), stop=(c == DC - 1))
                    last.then_inc(S["v_full"], 1)
                if p1 is not None:
                    transpose_exp(1, p1, b1, t, k)
                if p0 is not None:
                    passed(pe, "u0_done", p0)
                    passed(pe, "u1_done", p0)
                    bank_free(pe, "x1_done", t, k)
                    for g in range(G):
                        for c in range(DC):
                            for half_ in range(2):
                                last = pe.matmul(bank_of("x1_done")[:, g * D:(g + 1) * D], ut[:, b0_, g, c, half_ * P:(half_ + 1) * P],
                                                 w0_sb[:, (1 - half_) * DC + c, :], start=(c == 0 and half_ == 0), stop=(c == DC - 1 and half_ == 1))
                    last.then_inc(S["x1_full"], 1)
                if p2 is not None:
                    transpose_exp(2, p2, b2, t, k)
                if p3_ is not None:
                    passed(pe, "qt_done", p3_)
                    passed(pe, "kt_done", p3_)
                    passed(pe, "scores_masked", p3_, 1)
                    for c in range(DC):
                        for g in range(G):
                            for j in range(HPC):
                                r = slice(j * DH, (j + 1) * DH)
                                last = pe.matmul(score_bank[j][:, (c * G + g) * P:(c * G + g + 1) * P], qt[r, b3, c, g * P:(g + 1) * P],
                                                 kt[r, b3, c, g * P:(g + 1) * P], start=True, stop=True, tile_position=(j * DH, 0))
                    last.then_inc(S["scores_full"], 1)
                if p1 is not None:
                    passed(pe, "at1_done", p1)
                    bank_free(pe, "x2_done", t, k)
                    for g in range(G):
                        last = pe.matmul(bank_of("x2_done")[:, g * D:(g + 1) * D], at[1][:, b1, g], wh[:, b1, g, 0:D], start=True, stop=True)
                    last.then_inc(S["x2_full"], 1)
                if p2 is not None:
                    passed(pe, "at2_done", p2)
                    bank_free(pe, "x3_done", t, k)
                    for g in range(G):
                        last = pe.matmul(bank_of("x3_done")[:, g * F1:(g + 1) * F1], at[2][:, b2, g], hh[:, b2, g, 0:F1], start=True, stop=True)
                    last.then_inc(S["x3_full"], 1)

            run_steps(pe, step)


def kernel(x, adj, L0_gnn_W, L0_gnn_b, L1_gnn_W, L1_gnn_a_src, L1_gnn_a_dst, L2_gnn_W, L2_gnn_a, L3_gnn_Wq, L3_gnn_bq,
           L3_gnn_Wk, L3_gnn_bk, L3_gnn_Wv, L3_gnn_bv, L3_gnn_Wo, L3_gnn_bo):
    import numpy as np
    import concourse.bacc as bacc
    from concourse.bass_utils import run_bass_kernel_spmd

    def columns(b):
        return np.asarray(b).reshape(DC, P).T

    ins = {
        "x": x, "adj": adj, "w0t": np.asarray(L0_gnn_W).T, "b0": L0_gnn_b,
        "w1": L1_gnn_W, "w1t": np.asarray(L1_gnn_W).T,
        "a1": np.stack([np.asarray(L1_gnn_a_src), np.asarray(L1_gnn_a_dst)], axis=1),
        "w2": L2_gnn_W, "w2t": np.asarray(L2_gnn_W).T, "a2": np.asarray(L2_gnn_a)[:, :, 0].T,
        "wqt": np.asarray(L3_gnn_Wq).T, "bq": columns(L3_gnn_bq),
        "wkt": np.asarray(L3_gnn_Wk).T, "bk": columns(L3_gnn_bk),
        "wvt": np.asarray(L3_gnn_Wv).T, "bv": columns(L3_gnn_bv),
        "wot": np.asarray(L3_gnn_Wo).T, "bo": L3_gnn_bo,
    }
    nc = bacc.Bacc("TRN2", target_bir_lowering=False, num_devices=1)
    arrays, args = {}, []
    for name, a in ins.items():
        arrays[f"in_{name}"] = a = np.ascontiguousarray(a)
        args.append(nc.dram_tensor(f"in_{name}", a.shape, mybir.dt.from_np(a.dtype), kind="ExternalInput").ap())
    args.append(nc.dram_tensor("out", arrays["in_x"].shape, F32, kind="ExternalOutput").ap())
    gnn_kernel(nc, *args)
    r = run_bass_kernel_spmd(nc, [arrays], core_ids=[0])
    return r.results[0]["out"]
```

```python
from contextlib import ExitStack

import concourse.bass as bass
from concourse import mybir

F32 = mybir.dt.float32
F32R = mybir.dt.float32r
BF16 = mybir.dt.bfloat16
I32 = mybir.dt.int32
ALU = mybir.AluOpType
ACT = mybir.ActivationFunctionType
AX = mybir.AxisListType

P = 128
D = 256
DC = D // P
G = 2
F1 = 128
HEADS = 8
DH = D // HEADS
HPC = P // DH
NH = G * HEADS
LN_EPS = 1e-5
SLOPE = 0.2
MASKED = -1e30
NEG = 1e9

FIRST_LOOPED = 6
LAG = {"load": -2, "pre": -1, "l0": 0, "l1": 1, "l2": 2, "l3": 3, "l3b": 4}

BANK_TASKS = ["u0_done", "u1_done", "h1t_done", "pt0_done", "pt1_done", "pt2_done", "pt3_done", "wh0_done",
              "wh1_done", "ot_done", "h2t_done", "h3t_done", "d1_done", "hh_done", "qt_done", "kt_done",
              "d2_done", "v_done", "at1_done", "at2_done", "x1_done", "x2_done", "x3_done", "x4_done"]
TASK_LAG = {"u0_done": 0, "u1_done": 0, "x1_done": 0,
            "h1t_done": 1, "wh0_done": 1, "wh1_done": 1, "d1_done": 1, "at1_done": 1, "x2_done": 1,
            "h2t_done": 2, "hh_done": 2, "d2_done": 2, "at2_done": 2, "x3_done": 2,
            "h3t_done": 3, "qt_done": 3, "kt_done": 3, "v_done": 3,
            "pt0_done": 4, "pt1_done": 4, "pt2_done": 4, "pt3_done": 4, "ot_done": 4, "x4_done": 4}
NBANKS = 4
assert len(BANK_TASKS) % NBANKS == 0


class Looped:

    def __init__(self, t, offset):
        self.t, self.offset = t, offset


def gnn_kernel(nc, x, adj, w0t, b0, w1, w1t, a1, w2, w2t, a2, wqt, bq, wkt, bk, wvt, bv, wot, bo, out):
    NP = x.shape[0] // G
    last_looped = FIRST_LOOPED + (NP - 2 - FIRST_LOOPED) // 2 * 2
    last_step = NP + LAG["l3b"]

    x_pairs = x.rearrange("(p g) n d -> p n g d", g=G)
    out_pairs = out.rearrange("(p g) n d -> p n g d", g=G)

    with ExitStack() as ctx:
        def sb(name, shape, dt=F32):
            return ctx.enter_context(nc.sbuf_tensor(name, shape, dt))

        def sem(name):
            return ctx.enter_context(nc.semaphore(name))

        adj_i = sb("adj_i", [P, P], I32)
        adj_f = sb("adj_f", [P, P])
        ident = sb("ident", [P, P])
        deg = sb("deg", [P, 1])
        mask = sb("mask", [P, P])
        mask_bf = sb("mask_bf", [P, P], BF16)
        ident_bf = sb("ident_bf", [P, P], BF16)
        mask2 = sb("mask2", [P, P])
        has_any = sb("has_any", [P, 1])
        nan_row = sb("nan_row", [P, 1])
        eps = sb("eps", [P, G])
        minus_one = sb("minus_one", [P, G])
        half = sb("half", [P, G])
        aggr_r = sb("aggr_r", [P, 2 * P], F32R)
        w0_sb = sb("w0_sb", [P, 2 * DC, D])
        w1_sb = sb("w1_sb", [P, DC, D + 2])
        w1t_sb = sb("w1t_sb", [P, DC, D])
        a1_sb = sb("a1_sb", [P, DC, 2])
        w2_sb = sb("w2_sb", [P, DC, F1 + 2])
        w2t_sb = sb("w2t_sb", [P, D])
        a2_sb = sb("a2_sb", [P, 2])
        wq_sb = sb("wq_sb", [P, DC, D])
        wk_sb = sb("wk_sb", [P, DC, D])
        wv_sb = sb("wv_sb", [P, DC, D])
        wo_sb = sb("wo_sb", [P, DC, D])
        w0_r = [sb(f"w0_{part}", [P, 2 * DC, D], F32R) for part in ("hi", "lo")]
        wq_r = [sb(f"wq_{part}", [P, DC, D], F32R) for part in ("hi", "lo")]
        wk_r = [sb(f"wk_{part}", [P, DC, D], F32R) for part in ("hi", "lo")]
        wv_r = [sb(f"wv_{part}", [P, DC, D], F32R) for part in ("hi", "lo")]
        bq_sb = sb("bq_sb", [P, DC])
        bk_sb = sb("bk_sb", [P, DC])
        bv_sb = sb("bv_sb", [P, DC])
        deg_b = sb("deg_b", [P, D])
        c3 = sb("c3", [P, D])

        x0 = sb("x0", [P, 2, G, D])
        r0 = sb("r0", [P, 2, G, D])
        h0 = sb("h0", [P, 2, G, D])
        h0_r = [sb(f"h0_{part}", [P, 2, G, D], F32R) for part in ("hi", "lo")]
        ut_r = [sb(f"ut_{part}", [P, 2, G, DC, 2 * P], F32R) for part in ("hi", "lo")]
        x1 = sb("x1", [P, 2, G, D])
        x2 = sb("x2", [P, 2, G, D])
        x3 = sb("x3", [P, 2, G, D])
        r3 = sb("r3", [P, 2, G, D])
        x4 = sb("x4", [P, 2, G, D])
        y = [None] + [sb(f"y{i}", [P, 2, G, D]) for i in (1, 2, 3)]
        ht = [None] + [sb(f"ht{i}", [P, 2, DC, G, P]) for i in (1, 2)]
        ht3_r = [sb(f"ht3_{part}", [P, 2, DC, G, P], F32R) for part in ("hi", "lo")]
        wh = sb("wh", [P, 2, G, D + 2])
        hh = sb("hh", [P, 2, G, F1 + 2])
        z = [None] + [sb(f"z{i}", [P, 2, G, P]) for i in (1, 2)]
        ez = [None] + [sb(f"ez{i}", [P, 2, G, P]) for i in (1, 2)]
        at = [None] + [sb(f"at{i}", [P, 2, G, P]) for i in (1, 2)]
        stats = [sb(f"stats{i}", [P, 2, G, 6]) for i in range(4)]
        mv = [sb(f"mv{i}", [P, 2, G, 2]) for i in range(4)]
        rstd = [sb(f"rstd{i}", [P, 2, G]) for i in range(4)]
        veps = [sb(f"veps{i}", [P, 2, G]) for i in range(4)]
        negmean = sb("negmean", [P, 2, G])
        nmr = sb("nmr", [P, 2, G])
        nmax = [None] + [sb(f"nmax{i}", [P, 2, G]) for i in (1, 2)]
        ssum = [None] + [sb(f"ssum{i}", [P, 2, G]) for i in (1, 2)]
        rsum = [None] + [sb(f"rsum{i}", [P, 2, G]) for i in (1, 2)]
        qt = sb("qt", [P, 2, DC, G * P])
        kt = sb("kt", [P, 2, DC, G * P])
        v = sb("v", [P, 2, G, D])
        e3 = sb("e3", [P, HPC, DC * G, P])
        p3 = sb("p3", [P, HPC, DC * G, P])
        pt = sb("pt", [P, HPC, DC * G, P])
        nmax3 = sb("nmax3", [P, 2, HPC, DC * G])
        ssum3 = sb("ssum3", [P, 2, HPC, DC * G])
        rsum3 = sb("rsum3", [P, 2, HPC, DC * G])
        ot = sb("ot", [P, 2, DC, G * P])

        score_bank = [ctx.enter_context(nc.psum_tensor(f"score_bank{i}", [P, 512], F32)) for i in range(HPC)]
        general_bank = [ctx.enter_context(nc.psum_tensor(f"general_bank{i}", [P, 512], F32)) for i in range(NBANKS)]

        def bank_of(task):
            return general_bank[BANK_TASKS.index(task) % NBANKS]

        weights_in, adj_in = sem("weights_in"), sem("adj_in")
        c_pool, c_dve, c_pe, c_split = sem("c_pool"), sem("c_dve"), sem("c_pe"), sem("c_split")
        x_in = [sem("x_in_even"), sem("x_in_odd")]
        x_out = [sem("x_out_even"), sem("x_out_odd")]
        S = {}
        for name in BANK_TASKS:
            S[name] = sem(name)
        for name in ("u0_full", "u1_full", "x1_full", "h1t_full", "wh0_full", "wh1_full", "d1_full", "at1_full",
                     "x2_full", "h2t_full", "hh_full", "d2_full", "at2_full", "x3_full", "h3t_full", "qt_full",
                     "kt_full", "v_full", "pt0_full", "pt1_full", "pt2_full", "pt3_full", "ot_full", "x4_full",
                     "scores_full"):
            S[name] = sem(name)
        for i in range(4):
            S[f"stats{i}"] = sem(f"stats{i}")
            S[f"mv{i}"] = sem(f"mv{i}")
            S[f"veps{i}"] = sem(f"veps{i}")
            S[f"rstd{i}"] = sem(f"rstd{i}")
            if i:
                S[f"y{i}"] = sem(f"y{i}")
        for i in (1, 2):
            for name in ("lin", "leaky", "logit", "nmax", "exp", "rsum"):
                S[f"{name}{i}"] = sem(f"{name}{i}")
        for name in ("u0_hi", "u1_hi", "h3t_hi", "h0_hi", "h0_lo", "negmean", "nmr", "h0", "r0", "r3", "x3_tail", "rany1"):
            S[name] = sem(name)

        at_offset = {}

        for j in range(HPC):
            for name in ("nmax3", "exp3", "rsum3", "p3"):
                S[f"{name}_{j}"] = sem(f"{name}_{j}")

        def pair(t, k, stage):
            lag = LAG[stage]
            if isinstance(t, int) and not 0 <= t + k - lag < NP:
                return None, 0
            return (k - lag if isinstance(t, int) and t == 0 else Looped(t, k - lag)), (k - lag) % 2

        def passed(eng, name, p, back=0):
            if isinstance(p, Looped):
                eng.wait_ge(S[name], at_offset[p.offset + 1 - back])
            elif p - back >= 0:
                eng.wait_ge(S[name], p + 1 - back)

        def dma_count(p, b, back=0):
            return ((p - back) // 2 + 1) * 16 if isinstance(p, int) else (p.t + (p.offset + 2 - b - back)) * 8

        def index(p):
            return p if isinstance(p, int) else p.t + p.offset

        def bank_free(pe, task, t, k):
            i, back = BANK_TASKS.index(task) - NBANKS, 0
            while True:
                if i < 0:
                    i, back = i + len(BANK_TASKS), back + 1
                before = BANK_TASKS[i]
                lag = TASK_LAG[before]
                if not isinstance(t, int):
                    pe.wait_ge(S[before], at_offset[k - back - lag + 1])
                    return
                if t + k - back < LAG["load"]:
                    return
                if 0 <= t + k - back - lag < NP:
                    pe.wait_ge(S[before], t + k - back - lag + 1)
                    return
                i -= NBANKS

        def run_steps(eng, step):
            for s in range(LAG["load"], FIRST_LOOPED):
                step(0, s)
            with eng.Fori(FIRST_LOOPED, last_looped - 1, 2) as t:
                at_offset.clear()
                for offset in range(-FIRST_LOOPED + 1, 5):
                    at_offset[offset] = eng.snap(eng.to_reg(t + offset))
                step(t, 0)
                step(t, 1)
            for s in range(last_looped, last_step):
                step(0, s)

        block = ctx.enter_context(nc.Block())

        @block.sync
        def _(sp):
            sp.dma_start(adj_i[:], adj).then_inc(adj_in, 16)

            def load(p, b):
                if not isinstance(p, int) or p >= 2:
                    passed(sp, "h0_hi", p, 2)
                    passed(sp, "r0", p, 2)
                sp.dma_start(x0[:, b], x_pairs[bass.ds(index(p), 1)].rearrange("o n g d -> (o n) g d")).then_inc(x_in[b], 16)

            def step(t, k):
                p, b = pair(t, k, "load")
                if p is not None and not (isinstance(p, int) and p < 2):
                    load(p, b)
                p, b = pair(t, k, "l3b")
                if p is not None:
                    passed(sp, "x4_done", p)
                    sp.dma_start(out_pairs[bass.ds(index(p), 1)].rearrange("o n g d -> (o n) g d"), x4[:, b]).then_inc(x_out[b], 16)

            load(0, 0)
            load(1, 1)
            for dst, src in ((w0_sb[:], w0t.rearrange("(c p) o -> p c o", p=P)),
                             (deg_b[:], b0.partition_broadcast(P)),
                             (w1_sb[:, :, 0:D], w1.rearrange("(c p) o -> p c o", p=P)),
                             (w1t_sb[:], w1t.rearrange("(c p) o -> p c o", p=P)),
                             (a1_sb[:], a1.rearrange("(c p) o -> p c o", p=P)),
                             (w2_sb[:, :, 0:F1], w2.rearrange("(c p) o -> p c o", p=P)),
                             (w2t_sb[:], w2t), (a2_sb[:], a2),
                             (wq_sb[:], wqt.rearrange("(c p) o -> p c o", p=P)),
                             (wk_sb[:], wkt.rearrange("(c p) o -> p c o", p=P)),
                             (wv_sb[:], wvt.rearrange("(c p) o -> p c o", p=P)),
                             (wo_sb[:], wot.rearrange("(c p) o -> p c o", p=P)),
                             (bq_sb[:], bq), (bk_sb[:], bk), (bv_sb[:], bv),
                             (c3[:], bo.partition_broadcast(P))):
                sp.dma_start(dst, src).then_inc(weights_in, 16)

            run_steps(sp, step)
            sp.wait_ge(x_out[0], 16 * (NP // 2))
            sp.wait_ge(x_out[1], 16 * (NP // 2))

        n_weights = 16

        @block.gpsimd
        def _(pool):
            pool.memset(half[:], -0.5).then_inc(c_pool, 1)
            pool.memset(eps[:], LN_EPS)
            pool.memset(minus_one[:], -1.0)
            pool.memset(ident[:], 0.0).then_inc(c_pool, 1)
            pool.wait_ge(c_pool, 2)
            pool.affine_select(out=ident[:], in_=ident[:], compare_op=ALU.not_equal, fill=1.0, base=0,
                               pattern=[[-1, P]], channel_multiplier=1).then_inc(c_pool, 1)
            pool.wait_ge(c_dve, 8)

            def norm_scale(i, p, b):
                passed(pool, f"mv{i}", p)
                passed(pool, "h0_hi" if i == 0 else f"y{i}", p, 2)
                pool.tensor_tensor(veps[i][:, b], mv[i][:, b, :, 1], eps[:], ALU.add).then_inc(S[f"veps{i}"], 1)
                passed(pool, f"veps{i}", p)
                pool.tensor_tensor(rstd[i][:, b], veps[i][:, b], half[:], ALU.pow).then_inc(S[f"rstd{i}"], 1)

            def normalise_p3(j, p, b):
                passed(pool, f"rsum3_{j}", p)
                passed(pool, f"exp3_{j}", p)
                passed(pool, f"pt{j}_full", p, 1)
                pool.tensor_tensor(p3[:, j], e3[:, j], rsum3[:, b, j].unsqueeze(2).to_broadcast([P, DC * G, P]),
                                   ALU.mult).then_inc(S[f"p3_{j}"], 1)

            def step(t, k):
                pp, bp = pair(t, k, "pre")
                p0, b0_ = pair(t, k, "l0")
                p1, b1 = pair(t, k, "l1")
                p2, b2 = pair(t, k, "l2")
                p3_, b3 = pair(t, k, "l3")
                p4, b4 = pair(t, k, "l3b")
                if p3_ is not None:
                    passed(pool, "x4_done", p3_, 2)
                    passed(pool, "x3_done", p3_)
                    pool.tensor_tensor(r3[:, b3], x3[:, b3], c3[:].unsqueeze(1).to_broadcast([P, G, D]),
                                       ALU.add).then_inc(S["r3"], 1)
                if pp is not None:
                    norm_scale(0, pp, bp)
                    passed(pool, "h0_hi", pp, 2)
                    pool.tensor_tensor(negmean[:, bp], mv[0][:, bp, :, 0], minus_one[:], ALU.mult).then_inc(S["negmean"], 1)
                    passed(pool, "negmean", pp)
                    passed(pool, "rstd0", pp)
                    pool.tensor_tensor(nmr[:, bp], negmean[:, bp], rstd[0][:, bp], ALU.mult).then_inc(S["nmr"], 1)
                    pool.wait_ge(x_in[bp], dma_count(pp, bp))
                    passed(pool, "x1_done", pp, 2)
                    pool.tensor_tensor(r0[:, bp], x0[:, bp], deg_b[:].unsqueeze(1).to_broadcast([P, G, D]),
                                       ALU.add).then_inc(S["r0"], 1)
                if pp is not None:
                    passed(pool, "h0_hi", pp)
                    passed(pool, "h0", pp)
                    passed(pool, "u1_full", pp, 2)
                    pool.tensor_tensor(h0_r[1][:, bp], h0[:, bp], h0_r[0][:, bp].bitcast(F32), ALU.subtract).then_inc(S["h0_lo"], 1)
                if p2 is not None:
                    passed(pool, "hh_done", p2)
                    passed(pool, "y3", p2, 2)
                    passed(pool, "r3", p2, 2)
                    pool.tensor_tensor(x3[:, b2, :, F1:D], x2[:, b2, :, F1:D], hh[:, b2, :, 0:F1],
                                       ALU.add).then_inc(S["x3_tail"], 1)
                if p3_ is not None:
                    normalise_p3(0, p3_, b3)
                    normalise_p3(1, p3_, b3)
                if p0 is not None:
                    norm_scale(1, p0, b0_)
                if p3_ is not None:
                    normalise_p3(2, p3_, b3)
                    normalise_p3(3, p3_, b3)
                if p1 is not None:
                    norm_scale(2, p1, b1)
                if p2 is not None:
                    norm_scale(3, p2, b2)

            run_steps(pool, step)

        @block.vector
        def _(dve):
            dve.wait_ge(adj_in, 16)
            dve.tensor_copy(adj_f[:], adj_i[:]).then_inc(c_dve, 1)
            dve.wait_ge(c_dve, 1)
            dve.reduce_sum(deg[:], adj_f[:], AX.X).then_inc(c_dve, 1)
            dve.tensor_scalar(mask[:], adj_f[:], 0.0, MASKED, ALU.is_equal, ALU.mult).then_inc(c_dve, 1)
            dve.tensor_scalar(mask2[:], adj_f[:], 1.0, NEG, ALU.subtract, ALU.mult)
            dve.wait_ge(c_dve, 3)
            dve.wait_ge(c_pool, 3)
            dve.tensor_copy(mask_bf[:], mask[:])
            dve.tensor_copy(ident_bf[:], ident[:])
            dve.tensor_scalar(aggr_r[:, P:2 * P], ident[:], deg[:], None, ALU.mult)
            dve.wait_ge(weights_in, 16 * n_weights)
            dve.tensor_scalar(deg_b[:], deg_b[:], deg[:], None, ALU.mult)
            dve.reduce_max(has_any[:], mask[:], AX.X).then_inc(c_dve, 1)
            dve.wait_ge(c_dve, 4)
            dve.tensor_scalar(has_any[:], has_any[:], 0.0, None, ALU.is_equal).then_inc(c_dve, 1)
            dve.wait_ge(c_dve, 5)
            dve.reciprocal(nan_row[:], has_any[:]).then_inc(c_dve, 1)
            dve.wait_ge(c_dve, 6)
            dve.tensor_scalar(nan_row[:], nan_row[:], 0.0, None, ALU.mult).then_inc(c_dve, 1)
            for w, (hi, lo) in ((w0_sb, w0_r), (wq_sb, wq_r), (wk_sb, wk_r), (wv_sb, wv_r)):
                last = dve.tensor_copy(hi[:], w[:])
            last.then_inc(c_split, 1)
            dve.wait_ge(c_split, 1)
            for w, (hi, lo) in ((w0_sb, w0_r), (wq_sb, wq_r), (wk_sb, wk_r), (wv_sb, wv_r)):
                dve.tensor_tensor(lo[:], w[:], hi[:].bitcast(F32), ALU.subtract)
            dve.wait_ge(c_pe, 1)
            dve.wait_ge(c_dve, 7)
            dve.tensor_copy(aggr_r[:, 0:P], general_bank[0][:, 0:P])
            for c in range(DC):
                dve.tensor_copy(w1_sb[:, c, D:D + 2], general_bank[1][:, 2 * c:2 * c + 2])
                dve.tensor_copy(w2_sb[:, c, F1:F1 + 2], general_bank[2][:, 2 * c:2 * c + 2])
            dve.scalar_tensor_tensor(c3[:], general_bank[3][:, 0:D], nan_row[:], c3[:], ALU.add, ALU.add).then_inc(c_dve, 1)

            def norm_stats(i, src, p, b):
                passed(dve, f"rstd{i}", p, 2)
                if i == 0:
                    passed(dve, "negmean", p, 2)
                passed(dve, "h0_hi" if i == 0 else f"y{i}", p, 2)
                for g in range(G):
                    last = dve.bn_stats(stats[i][:, b, g], src[:, b, g])
                last.then_inc(S[f"stats{i}"], 1)
                dve.wait_ge(c_dve, 8)
                passed(dve, f"stats{i}", p)
                for g in range(G):
                    last = dve.bn_aggr(mv[i][:, b, g], stats[i][:, b, g])
                last.then_inc(S[f"mv{i}"], 1)

            def normalise(i, src, p, b):
                passed(dve, f"rstd{i}", p)
                passed(dve, f"mv{i}", p)
                passed(dve, f"h{i}t_full", p, 2)
                for g in range(G):
                    last = dve.tensor_scalar(y[i][:, b, g], src[:, b, g], mv[i][:, b, g, 0:1], rstd[i][:, b, g:g + 1],
                                             ALU.subtract, ALU.mult)
                last.then_inc(S[f"y{i}"], 1)

            def logits(i, msk, p, b):
                passed(dve, f"d{i}_done", p)
                dve.scalar_tensor_tensor(z[i][:, b], z[i][:, b], SLOPE, z[i][:, b], ALU.mult, ALU.max).then_inc(S[f"leaky{i}"], 1)
                passed(dve, f"leaky{i}", p)
                dve.tensor_tensor(z[i][:, b], z[i][:, b], msk[:].unsqueeze(1).to_broadcast([P, G, P]), ALU.add).then_inc(S[f"logit{i}"], 1)
                passed(dve, f"logit{i}", p)
                dve.tensor_reduce(nmax[i][:, b], z[i][:, b], AX.X, ALU.max, negate=True).then_inc(S[f"nmax{i}"], 1)

            def reciprocal3(j, p, b):
                passed(dve, f"exp3_{j}", p)
                passed(dve, f"p3_{j}", p, 2)
                dve.reciprocal(rsum3[:, b, j], ssum3[:, b, j]).then_inc(S[f"rsum3_{j}"], 1)

            def scores(j, p, b):
                passed(dve, "scores_full", p)
                passed(dve, f"exp3_{j}", p, 2)
                dve.tensor_reduce(nmax3[:, b, j], score_bank[j][:].rearrange("p (b n) -> p b n", n=P), AX.X, ALU.max,
                                  negate=True).then_inc(S[f"nmax3_{j}"], 1)

            def low_u(g, p, b):
                passed(dve, f"u{g}_hi", p)
                passed(dve, "x1_full", p, 2)
                dve.tensor_tensor(ut_r[1][:, b, g].rearrange("p c n -> p (c n)"), bank_of(f"u{g}_done")[:],
                                  ut_r[0][:, b, g].rearrange("p c n -> p (c n)").bitcast(F32), ALU.subtract).then_inc(S[f"u{g}_done"], 1)

            def add_bias(name, dst, bias, scale, p, b):
                passed(dve, f"{name}_full", p)
                passed(dve, "scores_full", p, 2)
                for c in range(DC):
                    last = dve.tensor_scalar(dst[:, b, c], bank_of(f"{name}_done")[:, c * G * P:(c + 1) * G * P], bias[:, c:c + 1], scale,
                                             ALU.add, ALU.mult)
                last.then_inc(S[f"{name}_done"], 1)

            def step(t, k):
                pp, bp = pair(t, k, "pre")
                p0, b0_ = pair(t, k, "l0")
                p1, b1 = pair(t, k, "l1")
                p2, b2 = pair(t, k, "l2")
                p3_, b3 = pair(t, k, "l3")
                p4, b4 = pair(t, k, "l3b")
                if pp is not None:
                    dve.wait_ge(x_in[bp], dma_count(pp, bp))
                    norm_stats(0, x0, pp, bp)
                if p4 is not None:
                    passed(dve, "ot_full", p4)
                    passed(dve, "x4_full", p4, 2)
                    dve.tensor_copy(ot[:, b4].rearrange("p c n -> p (c n)"), bank_of("ot_done")[:]).then_inc(S["ot_done"], 1)
                if p3_ is not None:
                    passed(dve, "h3t_hi", p3_)
                    passed(dve, "v_full", p3_, 2)
                    dve.scalar_tensor_tensor(ht3_r[1][:, b3].rearrange("p c g n -> p (c g n)"), bank_of("h3t_done")[:], 0.0,
                                             ht3_r[0][:, b3].rearrange("p c g n -> p (c g n)").bitcast(F32),
                                             ALU.max, ALU.subtract).then_inc(S["h3t_done"], 1)
                if p1 is not None:
                    logits(1, mask, p1, b1)
                if p3_ is not None:
                    add_bias("qt", qt, bq_sb, float(DH) ** -0.5, p3_, b3)
                if p3_ is not None:
                    add_bias("kt", kt, bk_sb, 1.0, p3_, b3)
                if p2 is not None:
                    logits(2, mask2, p2, b2)
                if p1 is not None:
                    passed(dve, "exp1", p1)
                    passed(dve, "x2_done", p1, 2)
                    dve.reciprocal(rsum[1][:, b1], ssum[1][:, b1]).then_inc(S["rany1"], 1)
                    passed(dve, "rany1", p1)
                    dve.tensor_scalar(rsum[1][:, b1], rsum[1][:, b1], has_any[:], None, ALU.mult).then_inc(S["rsum1"], 1)
                if p3_ is not None:
                    scores(0, p3_, b3)
                    scores(1, p3_, b3)
                if p3_ is not None:
                    scores(2, p3_, b3)
                    scores(3, p3_, b3)
                if p2 is not None:
                    passed(dve, "exp2", p2)
                    passed(dve, "x3_done", p2, 2)
                    dve.reciprocal(rsum[2][:, b2], ssum[2][:, b2]).then_inc(S["rsum2"], 1)
                if p3_ is not None:
                    reciprocal3(0, p3_, b3)
                    reciprocal3(1, p3_, b3)
                if p0 is not None:
                    passed(dve, "x1_full", p0)
                    passed(dve, "r0", p0)
                    passed(dve, "x2_done", p0, 2)
                    passed(dve, "y1", p0, 2)
                    dve.tensor_tensor(x1[:, b0_].rearrange("p g d -> p (g d)"), bank_of("x1_done")[:],
                                      r0[:, b0_].rearrange("p g d -> p (g d)"), ALU.add).then_inc(S["x1_done"], 1)
                    passed(dve, "x1_done", p0)
                    norm_stats(1, x1, p0, b0_)
                if p3_ is not None:
                    reciprocal3(2, p3_, b3)
                if p1 is not None:
                    passed(dve, "x2_full", p1)
                    passed(dve, "rsum1", p1)
                    passed(dve, "x3_done", p1, 2)
                    passed(dve, "x3_tail", p1, 2)
                    passed(dve, "y2", p1, 2)
                    for g in range(G):
                        last = dve.scalar_tensor_tensor(x2[:, b1, g], bank_of("x2_done")[:, g * D:(g + 1) * D], rsum[1][:, b1, g:g + 1],
                                                        x1[:, b1, g], ALU.mult, ALU.add)
                    last.then_inc(S["x2_done"], 1)
                if p2 is not None:
                    passed(dve, "x3_full", p2)
                    passed(dve, "rsum2", p2)
                    passed(dve, "y3", p2, 2)
                    passed(dve, "r3", p2, 2)
                    for g in range(G):
                        last = dve.scalar_tensor_tensor(x3[:, b2, g, 0:F1], bank_of("x3_done")[:, g * F1:(g + 1) * F1], rsum[2][:, b2, g:g + 1],
                                                        x2[:, b2, g, 0:F1], ALU.mult, ALU.add)
                    last.then_inc(S["x3_done"], 1)
                if p0 is not None:
                    normalise(1, x1, p0, b0_)
                if p3_ is not None:
                    reciprocal3(3, p3_, b3)
                if p4 is not None:
                    passed(dve, "x4_full", p4)
                    passed(dve, "r3", p4)
                    if not isinstance(p4, int) or p4 >= 2:
                        dve.wait_ge(x_out[b4], dma_count(p4, b4, 2))
                    dve.tensor_tensor(x4[:, b4].rearrange("p g d -> p (g d)"), bank_of("x4_done")[:],
                                      r3[:, b4].rearrange("p g d -> p (g d)"), ALU.add).then_inc(S["x4_done"], 1)
                if pp is not None:
                    low_u(0, pp, bp)
                    low_u(1, pp, bp)
                if p1 is not None:
                    passed(dve, "x2_done", p1)
                    norm_stats(2, x2, p1, b1)
                if p2 is not None:
                    passed(dve, "x3_done", p2)
                    passed(dve, "x3_tail", p2)
                    norm_stats(3, x3, p2, b2)
                if p1 is not None:
                    normalise(2, x2, p1, b1)
                if p2 is not None:
                    normalise(3, x3, p2, b2)

            run_steps(dve, step)

        @block.scalar
        def _(act):
            act.wait_ge(weights_in, 16 * n_weights)

            def exps(i, p, b):
                passed(act, f"nmax{i}", p)
                passed(act, f"at{i}_full", p, 2)
                passed(act, f"rsum{i}", p, 2)
                for g in range(G):
                    last = act.activation(ez[i][:, b, g], z[i][:, b, g], ACT.Exp, bias=nmax[i][:, b, g:g + 1],
                                          accum_out=ssum[i][:, b, g:g + 1])
                last.then_inc(S[f"exp{i}"], 1)

            def sum_logits(i, src, scol, p, b):
                passed(act, f"d{i}_full", p)
                passed(act, f"exp{i}", p, 2)
                bank = bank_of(f"d{i}_done")
                for g in range(G):
                    last = act.activation(z[i][:, b, g], bank[:, g * P:(g + 1) * P], ACT.Identity, bias=src[:, b, g, scol:scol + 1])
                last.then_inc(S[f"d{i}_done"], 1)

            def relu_transposed(i, p, b, reader):
                passed(act, f"h{i}t_full", p)
                passed(act, reader, p, 2)
                act.activation(ht[i][:, b].rearrange("p c g n -> p (c g n)"), bank_of(f"h{i}t_done")[:], ACT.Relu).then_inc(S[f"h{i}t_done"], 1)

            def copy_p3_transposed(j, p):
                passed(act, f"pt{j}_full", p)
                passed(act, "ot_full", p, 1)
                act.activation(pt[:, j].rearrange("p b n -> p (b n)"), bank_of(f"pt{j}_done")[:], ACT.Copy).then_inc(S[f"pt{j}_done"], 1)

            def exp_transposed(i, p, b):
                passed(act, f"at{i}_full", p)
                passed(act, f"x{i + 1}_full", p, 2)
                act.activation(at[i][:, b].rearrange("p g n -> p (g n)"), bank_of(f"at{i}_done")[:, 0:G * P], ACT.Copy).then_inc(S[f"at{i}_done"], 1)

            def copy_projection1(g, p, b):
                passed(act, f"wh{g}_full", p)
                passed(act, "x2_full", p, 2)
                passed(act, "d1_done", p, 2)
                act.activation(wh[:, b, g], bank_of(f"wh{g}_done")[:, 0:D + 2], ACT.Copy).then_inc(S[f"wh{g}_done"], 1)

            def exps3(j, p, b):
                passed(act, f"nmax3_{j}", p)
                passed(act, f"p3_{j}", p, 1)
                passed(act, f"rsum3_{j}", p, 2)
                for i in range(DC * G):
                    last = act.activation(e3[:, j, i], score_bank[j][:, i * P:(i + 1) * P], ACT.Exp, bias=nmax3[:, b, j, i:i + 1],
                                          accum_out=ssum3[:, b, j, i:i + 1])
                last.then_inc(S[f"exp3_{j}"], 1)

            def step(t, k):
                pp, bp = pair(t, k, "pre")
                p0, b0_ = pair(t, k, "l0")
                p1, b1 = pair(t, k, "l1")
                p2, b2 = pair(t, k, "l2")
                p3_, b3 = pair(t, k, "l3")
                p4, b4 = pair(t, k, "l3b")
                if p0 is not None:
                    for g in range(G):
                        passed(act, f"u{g}_full", p0)
                        passed(act, "x1_full", p0, 2)
                        passed(act, f"u{g}_done", p0, 2)
                        act.activation(ut_r[0][:, b0_, g].rearrange("p c n -> p (c n)"), bank_of(f"u{g}_done")[:], ACT.Copy).then_inc(S[f"u{g}_hi"], 1)
                if p1 is not None:
                    relu_transposed(1, p1, b1, "wh1_full")
                if p4 is not None:
                    copy_p3_transposed(0, p4)
                    copy_p3_transposed(1, p4)
                if p4 is not None:
                    copy_p3_transposed(2, p4)
                    copy_p3_transposed(3, p4)
                if p1 is not None:
                    copy_projection1(0, p1, b1)
                if p1 is not None:
                    copy_projection1(1, p1, b1)
                if p2 is not None:
                    relu_transposed(2, p2, b2, "hh_full")
                if p3_ is not None:
                    passed(act, "h3t_full", p3_)
                    passed(act, "v_full", p3_, 2)
                    passed(act, "h3t_done", p3_, 2)
                    act.activation(ht3_r[0][:, b3].rearrange("p c g n -> p (c g n)"), bank_of("h3t_done")[:], ACT.Relu).then_inc(S["h3t_hi"], 1)
                if p1 is not None:
                    sum_logits(1, wh, D, p1, b1)
                if p2 is not None:
                    passed(act, "hh_full", p2)
                    passed(act, "x3_full", p2, 2)
                    passed(act, "d2_done", p2, 2)
                    passed(act, "x3_tail", p2, 2)
                    act.activation(hh[:, b2].rearrange("p g n -> p (g n)"), bank_of("hh_done")[:, 0:G * (F1 + 2)], ACT.Copy).then_inc(S["hh_done"], 1)
                if pp is not None:
                    passed(act, "u1_full", pp, 2)
                    passed(act, "h0_lo", pp, 2)
                    passed(act, "nmr", pp)
                    for g in range(G):
                        last = act.activation(h0[:, bp, g], x0[:, bp, g], ACT.Relu, bias=nmr[:, bp, g:g + 1], scale=rstd[0][:, bp, g:g + 1])
                    last.then_inc(S["h0"], 1)
                    passed(act, "h0_lo", pp, 2)
                    for g in range(G):
                        last = act.activation(h0_r[0][:, bp, g], x0[:, bp, g], ACT.Relu, bias=nmr[:, bp, g:g + 1], scale=rstd[0][:, bp, g:g + 1])
                    last.then_inc(S["h0_hi"], 1)
                if p1 is not None:
                    exps(1, p1, b1)
                if p2 is not None:
                    sum_logits(2, hh, F1, p2, b2)
                if p2 is not None:
                    exps(2, p2, b2)
                if p3_ is not None:
                    exps3(0, p3_, b3)
                    passed(act, "v_full", p3_)
                    passed(act, "ot_full", p3_, 2)
                    act.activation(v[:, b3].rearrange("p g d -> p (g d)"), bank_of("v_done")[:], ACT.Copy).then_inc(S["v_done"], 1)
                    exps3(1, p3_, b3)
                if p1 is not None:
                    exp_transposed(1, p1, b1)
                if p2 is not None:
                    exp_transposed(2, p2, b2)
                if p3_ is not None:
                    exps3(2, p3_, b3)
                    exps3(3, p3_, b3)

            run_steps(act, step)

        @block.tensor
        def _(pe):
            pe.wait_ge(c_pool, 3)
            pe.wait_ge(c_dve, 1)
            pe.wait_ge(weights_in, 16 * n_weights)
            pe.transpose(general_bank[0][:, 0:P], adj_f[:], ident[:])
            for c in range(DC):
                for e in range(DC):
                    pe.matmul(general_bank[1][:, 2 * c:2 * c + 2], w1t_sb[:, e, c * P:(c + 1) * P], a1_sb[:, e, :],
                              start=(e == 0), stop=(e == DC - 1))
                pe.matmul(general_bank[2][:, 2 * c:2 * c + 2], w2t_sb[:, c * P:(c + 1) * P], a2_sb[:], start=True, stop=True)
            for c in range(DC):
                last = pe.matmul(general_bank[3][:, 0:D], bv_sb[:, c:c + 1].to_broadcast([P, P]), wo_sb[:, c, :],
                                 start=(c == 0), stop=(c == DC - 1))
            last.then_inc(c_pe, 1)
            pe.wait_ge(c_dve, 8)

            def split_matmul(out_ap, lhs, rhs, start, stop):
                pe.matmul(out_ap, lhs[0], rhs[0], start=start, stop=False)
                pe.matmul(out_ap, lhs[0], rhs[1], start=False, stop=False)
                return pe.matmul(out_ap, lhs[1], rhs[0], start=False, stop=stop)

            def transpose_y(i, p, b, t, k):
                passed(pe, f"y{i}", p)
                bank_free(pe, f"h{i}t_done", t, k)
                for c in range(DC):
                    for g in range(G):
                        last = pe.transpose(bank_of(f"h{i}t_done")[:, (c * G + g) * P:(c * G + g + 1) * P], y[i][:, b, g, c * P:(c + 1) * P], ident[:])
                last.then_inc(S[f"h{i}t_full"], 1)

            def spread_dst(i, src, col, p, b, t, k):
                bank_free(pe, f"d{i}_done", t, k)
                for g in range(G):
                    last = pe.transpose(bank_of(f"d{i}_done")[:, g * P:(g + 1) * P], src[:, b, g, col:col + 1].to_broadcast([P, P]), ident[:])
                last.then_inc(S[f"d{i}_full"], 1)

            def transpose_exp(i, p, b, t, k):
                passed(pe, f"exp{i}", p)
                bank_free(pe, f"at{i}_done", t, k)
                for g in range(G):
                    last = pe.transpose(bank_of(f"at{i}_done")[:, g * P:(g + 1) * P], ez[i][:, b, g], ident[:])
                last.then_inc(S[f"at{i}_full"], 1)

            def project1(g, p, b, t, k):
                passed(pe, "h1t_done", p)
                bank_free(pe, f"wh{g}_done", t, k)
                for c in range(DC):
                    last = pe.matmul(bank_of(f"wh{g}_done")[:, 0:D + 2], ht[1][:, b, c, g], w1_sb[:, c, :], start=(c == 0), stop=(c == DC - 1))
                last.then_inc(S[f"wh{g}_full"], 1)

            def transpose_p3(j, p, b, t, k):
                passed(pe, f"p3_{j}", p)
                bank_free(pe, f"pt{j}_done", t, k)
                for i in range(DC * G):
                    last = pe.transpose(bank_of(f"pt{j}_done")[:, i * P:(i + 1) * P], p3[:, j, i], ident[:])
                last.then_inc(S[f"pt{j}_full"], 1)

            def step(t, k):
                p0, b0_ = pair(t, k, "l0")
                p1, b1 = pair(t, k, "l1")
                p2, b2 = pair(t, k, "l2")
                p3_, b3 = pair(t, k, "l3")
                p4, b4 = pair(t, k, "l3b")
                if p0 is not None:
                    passed(pe, "h0_hi", p0)
                    passed(pe, "h0_lo", p0)
                    for g in range(G):
                        bank_free(pe, f"u{g}_done", t, k)
                        for c in range(DC):
                            for part in range(2):
                                last = pe.matmul(bank_of(f"u{g}_done")[:, c * 2 * P:(c + 1) * 2 * P], h0_r[part][:, b0_, g, c * P:(c + 1) * P], aggr_r[:],
                                                 start=(part == 0), stop=(part == 1))
                        last.then_inc(S[f"u{g}_full"], 1)
                if p1 is not None:
                    transpose_y(1, p1, b1, t, k)
                if p4 is not None:
                    transpose_p3(0, p4, b4, t, k)
                    transpose_p3(1, p4, b4, t, k)
                if p4 is not None:
                    transpose_p3(2, p4, b4, t, k)
                    transpose_p3(3, p4, b4, t, k)
                if p1 is not None:
                    project1(0, p1, b1, t, k)
                if p1 is not None:
                    project1(1, p1, b1, t, k)
                if p4 is not None:
                    for j in range(HPC):
                        passed(pe, f"pt{j}_done", p4)
                    passed(pe, "v_done", p4)
                    bank_free(pe, "ot_done", t, k)
                    for c in range(DC):
                        for g in range(G):
                            for j in range(HPC):
                                last = pe.matmul(bank_of("ot_done")[j * DH:(j + 1) * DH, (c * G + g) * P:(c * G + g + 1) * P],
                                                 v[:, b4, g, c * P + j * DH:c * P + (j + 1) * DH], pt[:, j, c * G + g], start=True, stop=True, tile_position=(0, j * DH))
                    last.then_inc(S["ot_full"], 1)
                if p2 is not None:
                    transpose_y(2, p2, b2, t, k)
                if p3_ is not None:
                    transpose_y(3, p3_, b3, t, k)
                if p1 is not None:
                    passed(pe, "wh0_done", p1)
                    passed(pe, "wh1_done", p1)
                    spread_dst(1, wh, D + 1, p1, b1, t, k)
                if p2 is not None:
                    passed(pe, "h2t_done", p2)
                    bank_free(pe, "hh_done", t, k)
                    for g in range(G):
                        for c in range(DC):
                            last = pe.matmul(bank_of("hh_done")[:, g * (F1 + 2):(g + 1) * (F1 + 2)], ht[2][:, b2, c, g], w2_sb[:, c, :], start=(c == 0), stop=(c == DC - 1))
                    last.then_inc(S["hh_full"], 1)
                if p3_ is not None:
                    passed(pe, "h3t_done", p3_)
                    for name, w in (("qt", wq_r), ):
                        bank_free(pe, f"{name}_done", t, k)
                        for o in range(DC):
                            for c in range(DC):
                                last = split_matmul(bank_of(f"{name}_done")[:, o * G * P:(o + 1) * G * P], [w_[:, c, o * P:(o + 1) * P] for w_ in w],
                                                    [h_[:, b3, c].rearrange("p g n -> p (g n)") for h_ in ht3_r], c == 0, c == DC - 1)
                        last.then_inc(S[f"{name}_full"], 1)
                if p3_ is not None:
                    bank_free(pe, "kt_done", t, k)
                    for o in range(DC):
                        for c in range(DC):
                            last = split_matmul(bank_of("kt_done")[:, o * G * P:(o + 1) * G * P], [w_[:, c, o * P:(o + 1) * P] for w_ in wk_r],
                                                [h_[:, b3, c].rearrange("p g n -> p (g n)") for h_ in ht3_r], c == 0, c == DC - 1)
                    last.then_inc(S["kt_full"], 1)
                if p2 is not None:
                    passed(pe, "hh_done", p2)
                    spread_dst(2, hh, F1 + 1, p2, b2, t, k)
                if p3_ is not None:
                    for j in range(HPC):
                        passed(pe, f"exp3_{j}", p3_, 1)
                        pe.matmul(score_bank[j][:], ident_bf[:], mask_bf[:].unsqueeze(1).to_broadcast([P, DC * G, P]), start=True, stop=False)
                    passed(pe, "qt_done", p3_)
                    passed(pe, "kt_done", p3_)
                    for c in range(DC):
                        for g in range(G):
                            for j in range(HPC):
                                r = slice(j * DH, (j + 1) * DH)
                                last = pe.matmul(score_bank[j][:, (c * G + g) * P:(c * G + g + 1) * P], qt[r, b3, c, g * P:(g + 1) * P],
                                                 kt[r, b3, c, g * P:(g + 1) * P], start=False, stop=(c == DC - 1 and g == G - 1), tile_position=(j * DH, 0))
                    last.then_inc(S["scores_full"], 1)
                if p3_ is not None:
                    bank_free(pe, "v_done", t, k)
                    for g in range(G):
                        for c in range(DC):
                            last = split_matmul(bank_of("v_done")[:, g * D:(g + 1) * D], [h_[:, b3, c, g] for h_ in ht3_r],
                                                [w_[:, c, :] for w_ in wv_r], c == 0, c == DC - 1)
                    last.then_inc(S["v_full"], 1)
                if p1 is not None:
                    transpose_exp(1, p1, b1, t, k)
                if p2 is not None:
                    transpose_exp(2, p2, b2, t, k)
                if p0 is not None:
                    passed(pe, "u0_done", p0)
                    passed(pe, "u1_done", p0)
                    bank_free(pe, "x1_done", t, k)
                    for g in range(G):
                        for c in range(DC):
                            for half_ in range(2):
                                last = split_matmul(bank_of("x1_done")[:, g * D:(g + 1) * D], [u_[:, b0_, g, c, half_ * P:(half_ + 1) * P] for u_ in ut_r],
                                                    [w[:, (1 - half_) * DC + c, :] for w in w0_r], c == 0 and half_ == 0, c == DC - 1 and half_ == 1)
                    last.then_inc(S["x1_full"], 1)
                if p1 is not None:
                    passed(pe, "at1_done", p1)
                    bank_free(pe, "x2_done", t, k)
                    for g in range(G):
                        last = pe.matmul(bank_of("x2_done")[:, g * D:(g + 1) * D], at[1][:, b1, g], wh[:, b1, g, 0:D], start=True, stop=True)
                    last.then_inc(S["x2_full"], 1)
                if p2 is not None:
                    passed(pe, "at2_done", p2)
                    bank_free(pe, "x3_done", t, k)
                    for g in range(G):
                        last = pe.matmul(bank_of("x3_done")[:, g * F1:(g + 1) * F1], at[2][:, b2, g], hh[:, b2, g, 0:F1], start=True, stop=True)
                    last.then_inc(S["x3_full"], 1)
                if p4 is not None:
                    passed(pe, "ot_done", p4)
                    bank_free(pe, "x4_done", t, k)
                    for g in range(G):
                        for c in range(DC):
                            last = pe.matmul(bank_of("x4_done")[:, g * D:(g + 1) * D], ot[:, b4, c, g * P:(g + 1) * P], wo_sb[:, c, :], start=(c == 0), stop=(c == DC - 1))
                    last.then_inc(S["x4_full"], 1)

            run_steps(pe, step)


def kernel(x, adj, L0_gnn_W, L0_gnn_b, L1_gnn_W, L1_gnn_a_src, L1_gnn_a_dst, L2_gnn_W, L2_gnn_a, L3_gnn_Wq, L3_gnn_bq,
           L3_gnn_Wk, L3_gnn_bk, L3_gnn_Wv, L3_gnn_bv, L3_gnn_Wo, L3_gnn_bo):
    import numpy as np
    import concourse.bacc as bacc
    from concourse.bass_utils import run_bass_kernel_spmd

    def columns(b):
        return np.asarray(b).reshape(DC, P).T

    ins = {
        "x": x, "adj": adj, "w0t": np.asarray(L0_gnn_W).T, "b0": L0_gnn_b,
        "w1": L1_gnn_W, "w1t": np.asarray(L1_gnn_W).T,
        "a1": np.stack([np.asarray(L1_gnn_a_src), np.asarray(L1_gnn_a_dst)], axis=1),
        "w2": L2_gnn_W, "w2t": np.asarray(L2_gnn_W).T, "a2": np.asarray(L2_gnn_a)[:, :, 0].T,
        "wqt": np.asarray(L3_gnn_Wq).T, "bq": columns(L3_gnn_bq),
        "wkt": np.asarray(L3_gnn_Wk).T, "bk": columns(L3_gnn_bk),
        "wvt": np.asarray(L3_gnn_Wv).T, "bv": columns(L3_gnn_bv),
        "wot": np.asarray(L3_gnn_Wo).T, "bo": L3_gnn_bo,
    }
    nc = bacc.Bacc("TRN2", target_bir_lowering=False, num_devices=1)
    arrays, args = {}, []
    for name, a in ins.items():
        arrays[f"in_{name}"] = a = np.ascontiguousarray(a)
        args.append(nc.dram_tensor(f"in_{name}", a.shape, mybir.dt.from_np(a.dtype), kind="ExternalInput").ap())
    args.append(nc.dram_tensor("out", arrays["in_x"].shape, F32, kind="ExternalOutput").ap())
    gnn_kernel(nc, *args)
    r = run_bass_kernel_spmd(nc, [arrays], core_ids=[0])
    return r.results[0]["out"]
```

```python
from contextlib import ExitStack

import concourse.bass as bass
from concourse import mybir

F32 = mybir.dt.float32
F32R = mybir.dt.float32r
BF16 = mybir.dt.bfloat16
I32 = mybir.dt.int32
ALU = mybir.AluOpType
ACT = mybir.ActivationFunctionType
AX = mybir.AxisListType

P = 128
D = 256
DC = D // P
G = 2
F1 = 128
HEADS = 8
DH = D // HEADS
HPC = P // DH
NH = G * HEADS
LN_EPS = 1e-5
SLOPE = 0.2
MASKED = -1e30
NEG = 1e9

FIRST_LOOPED = 6
STAGE_LAG = {"load": -2, "pre": -1, "l0": 0, "l1": 1, "l2": 2, "l3": 3, "l3b": 4}

BANK_TASKS = ["x3_done", "pt0_done", "pt2_done", "pt3_done", "wh1_done", "pt1_done", "wh0_done", "ot_done",
              "h2t_done", "h3t_done", "d1_done", "hh_done", "kt_done", "qt_done", "d2_done", "at1_done",
              "x1_done", "at2_done", "v_done", "x2_done", "u1_done", "x4_done", "h1t_done", "u0_done"]
TASK_LAG = {"u1_done": -1, "u0_done": -1,
            "x1_done": 0, "h1t_done": 0,
            "wh1_done": 1, "wh0_done": 1, "d1_done": 1, "at1_done": 1, "x2_done": 1,
            "h2t_done": 2, "hh_done": 2, "d2_done": 2, "at2_done": 2,
            "x3_done": 3, "h3t_done": 3, "kt_done": 3, "qt_done": 3, "v_done": 3,
            "pt0_done": 4, "pt2_done": 4, "pt3_done": 4, "pt1_done": 4, "ot_done": 4, "x4_done": 4}
NBANKS = 4
assert len(BANK_TASKS) % NBANKS == 0


class Looped:

    def __init__(self, t, offset):
        self.t, self.offset = t, offset


def gnn_kernel(nc, x, adj, w0t, bias0, w1, w1t, a1, w2, w2t, a2, wqt, bq, wkt, bk, wvt, bv, wot, bo, out):
    NP = x.shape[0] // G
    last_looped = FIRST_LOOPED + (NP - 2 - FIRST_LOOPED) // 2 * 2
    last_step = NP + STAGE_LAG["l3b"]

    x_pairs = x.rearrange("(p g) n d -> p n g d", g=G)
    out_pairs = out.rearrange("(p g) n d -> p n g d", g=G)

    with ExitStack() as ctx:
        def sb(name, shape, dt=F32):
            return ctx.enter_context(nc.sbuf_tensor(name, shape, dt))

        def sem(name):
            return ctx.enter_context(nc.semaphore(name))

        adj_i = sb("adj_i", [P, P], I32)
        adj_f = sb("adj_f", [P, P])
        ident = sb("ident", [P, P])
        deg = sb("deg", [P, 1])
        mask = sb("mask", [P, P])
        mask_bf = sb("mask_bf", [P, P], BF16)
        ident_bf = sb("ident_bf", [P, P], BF16)
        mask2 = sb("mask2", [P, P])
        has_any = sb("has_any", [P, 1])
        nan_row = sb("nan_row", [P, 1])
        eps = sb("eps", [P, G])
        minus_one = sb("minus_one", [P, G])
        power = sb("power", [P, G])
        aggr_r = sb("aggr_r", [P, 2 * P], F32R)
        w0_sb = sb("w0_sb", [P, 2 * DC, D])
        w1_sb = sb("w1_sb", [P, DC, D + 2])
        w1t_sb = sb("w1t_sb", [P, DC, D])
        a1_sb = sb("a1_sb", [P, DC, 2])
        w2_sb = sb("w2_sb", [P, DC, F1 + 2])
        w2t_sb = sb("w2t_sb", [P, D])
        a2_sb = sb("a2_sb", [P, 2])
        wq_sb = sb("wq_sb", [P, DC, D])
        wk_sb = sb("wk_sb", [P, DC, D])
        wv_sb = sb("wv_sb", [P, DC, D])
        wo_sb = sb("wo_sb", [P, DC, D])
        w0_r = [sb(f"w0_{part}", [P, 2 * DC, D], F32R) for part in ("hi", "lo")]
        wq_r = [sb(f"wq_{part}", [P, DC, D], F32R) for part in ("hi", "lo")]
        wk_r = [sb(f"wk_{part}", [P, DC, D], F32R) for part in ("hi", "lo")]
        wv_r = [sb(f"wv_{part}", [P, DC, D], F32R) for part in ("hi", "lo")]
        w1_r = [sb(f"w1_{part}", [P, DC, D + 2], F32R) for part in ("hi", "lo")]
        wo_r = [sb(f"wo_{part}", [P, DC, D], F32R) for part in ("hi", "lo")]
        bq_sb = sb("bq_sb", [P, DC])
        bk_sb = sb("bk_sb", [P, DC])
        bv_sb = sb("bv_sb", [P, DC])
        deg_b = sb("deg_b", [P, D])
        c3 = sb("c3", [P, D])

        x0 = sb("x0", [P, 2, G, D])
        r0 = sb("r0", [P, 2, G, D])
        h0 = sb("h0", [P, 2, G, D])
        h0_r = [sb(f"h0_{part}", [P, 2, G, D], F32R) for part in ("hi", "lo")]
        ut_r = [sb(f"ut_{part}", [P, 2, G, DC, 2 * P], F32R) for part in ("hi", "lo")]
        x1 = sb("x1", [P, 2, G, D])
        x2 = sb("x2", [P, 2, G, D])
        x3 = sb("x3", [P, 2, G, D])
        r3 = sb("r3", [P, 2, G, D])
        x4 = sb("x4", [P, 2, G, D])
        y = [None] + [sb(f"y{i}", [P, 2, G, D]) for i in (1, 2, 3)]
        ht1_r = [sb(f"ht1_{part}", [P, 2, DC, G, P], F32R) for part in ("hi", "lo")]
        ht2 = sb("ht2", [P, 2, DC, G, P])
        ht3_r = [sb(f"ht3_{part}", [P, 2, DC, G, P], F32R) for part in ("hi", "lo")]
        wh = sb("wh", [P, 2, G, D + 2])
        hh = sb("hh", [P, 2, G, F1 + 2])
        z = [None] + [sb(f"z{i}", [P, 2, G, P]) for i in (1, 2)]
        ez = [None] + [sb(f"ez{i}", [P, 2, G, P]) for i in (1, 2)]
        at = [None] + [sb(f"at{i}", [P, 2, G, P]) for i in (1, 2)]
        stats = [sb(f"stats{i}", [P, 2, G, 6]) for i in range(4)]
        mv = [sb(f"mv{i}", [P, 2, G, 2]) for i in range(4)]
        rstd = [sb(f"rstd{i}", [P, 2, G]) for i in range(4)]
        veps = [sb(f"veps{i}", [P, 2, G]) for i in range(4)]
        negmean = sb("negmean", [P, 2, G])
        nmr = sb("nmr", [P, 2, G])
        nmax = [None] + [sb(f"nmax{i}", [P, 2, G]) for i in (1, 2)]
        ssum = [None] + [sb(f"ssum{i}", [P, 2, G]) for i in (1, 2)]
        rsum = [None] + [sb(f"rsum{i}", [P, 2, G]) for i in (1, 2)]
        qt = sb("qt", [P, 2, DC, G * P])
        kt = sb("kt", [P, 2, DC, G * P])
        v = sb("v", [P, 2, G, D])
        exps3_sb = sb("exps3_sb", [P, HPC, DC * G, P])
        probs3 = sb("probs3", [P, HPC, DC * G, P])
        probs3_t = sb("probs3_t", [P, HPC, DC * G, P])
        nmax3 = sb("nmax3", [P, 2, HPC, DC * G])
        ssum3 = sb("ssum3", [P, 2, HPC, DC * G])
        rsum3 = sb("rsum3", [P, 2, HPC, DC * G])
        ot_r = [sb(f"ot_{part}", [P, 2, DC, G * P], F32R) for part in ("hi", "lo")]

        score_bank = [ctx.enter_context(nc.psum_tensor(f"score_bank{i}", [P, 512], F32)) for i in range(HPC)]
        general_bank = [ctx.enter_context(nc.psum_tensor(f"general_bank{i}", [P, 512], F32)) for i in range(NBANKS)]

        def bank_of(task):
            return general_bank[BANK_TASKS.index(task) % NBANKS]

        weights_in, adj_in = sem("weights_in"), sem("adj_in")
        c_pool, c_dve, c_pe, c_split = sem("c_pool"), sem("c_dve"), sem("c_pe"), sem("c_split")
        x_in = [sem("x_in_even"), sem("x_in_odd")]
        x_out = [sem("x_out_even"), sem("x_out_odd")]
        S = {}
        for name in BANK_TASKS:
            S[name] = sem(name)
        for name in ("u0_full", "u1_full", "x1_full", "h1t_full", "wh0_full", "wh1_full", "d1_full", "at1_full",
                     "x2_full", "h2t_full", "hh_full", "d2_full", "at2_full", "x3_full", "h3t_full", "qt_full",
                     "kt_full", "v_full", "pt0_full", "pt1_full", "pt2_full", "pt3_full", "ot_full", "x4_full",
                     "scores_full"):
            S[name] = sem(name)
        for i in range(4):
            S[f"stats{i}"] = sem(f"stats{i}")
            S[f"mv{i}"] = sem(f"mv{i}")
            S[f"veps{i}"] = sem(f"veps{i}")
            S[f"rstd{i}"] = sem(f"rstd{i}")
            if i:
                S[f"y{i}"] = sem(f"y{i}")
        for i in (1, 2):
            for name in ("lin", "leaky", "logit", "nmax", "exp", "rsum"):
                S[f"{name}{i}"] = sem(f"{name}{i}")
        for name in ("u0_hi", "u1_hi", "h3t_hi", "h1t_hi", "ot_hi", "h0_hi", "h0_lo", "negmean", "nmr", "h0", "r0", "r3", "x3_tail", "rsum1_any"):
            S[name] = sem(name)

        at_offset = {}

        for j in range(HPC):
            for name in ("nmax3", "exp3", "rsum3", "p3"):
                S[f"{name}_{j}"] = sem(f"{name}_{j}")

        def pair(t, k, stage):
            lag = STAGE_LAG[stage]
            if isinstance(t, int) and not 0 <= t + k - lag < NP:
                return None, 0
            return (k - lag if isinstance(t, int) and t == 0 else Looped(t, k - lag)), (k - lag) % 2

        def passed(eng, name, p, back=0):
            if isinstance(p, Looped):
                eng.wait_ge(S[name], at_offset[p.offset + 1 - back])
            elif p - back >= 0:
                eng.wait_ge(S[name], p + 1 - back)

        def dma_count(p, b, back=0):
            return ((p - back) // 2 + 1) * 16 if isinstance(p, int) else (p.t + (p.offset + 2 - b - back)) * 8

        def index(p):
            return p if isinstance(p, int) else p.t + p.offset

        def bank_free(pe, task, t, k):
            i, back = BANK_TASKS.index(task) - NBANKS, 0
            while True:
                if i < 0:
                    i, back = i + len(BANK_TASKS), back + 1
                before = BANK_TASKS[i]
                lag = TASK_LAG[before]
                if not isinstance(t, int):
                    pe.wait_ge(S[before], at_offset[k - back - lag + 1])
                    return
                if t + k - back < STAGE_LAG["load"]:
                    return
                if 0 <= t + k - back - lag < NP:
                    pe.wait_ge(S[before], t + k - back - lag + 1)
                    return
                i -= NBANKS

        def run_steps(eng, step):
            for s in range(STAGE_LAG["load"], FIRST_LOOPED):
                step(0, s)
            with eng.Fori(FIRST_LOOPED, last_looped - 1, 2) as t:
                at_offset.clear()
                for offset in range(-FIRST_LOOPED + 1, 5):
                    at_offset[offset] = eng.snap(eng.to_reg(t + offset))
                step(t, 0)
                step(t, 1)
            for s in range(last_looped, last_step):
                step(0, s)

        block = ctx.enter_context(nc.Block())

        @block.sync
        def _(sp):
            sp.dma_start(adj_i[:], adj).then_inc(adj_in, 16)

            def load(p, b):
                if not isinstance(p, int) or p >= 2:
                    passed(sp, "h0_hi", p, 2)
                    passed(sp, "r0", p, 2)
                sp.dma_start(x0[:, b], x_pairs[bass.ds(index(p), 1)].rearrange("o n g d -> (o n) g d")).then_inc(x_in[b], 16)

            def step(t, k):
                p, b = pair(t, k, "load")
                if p is not None and not (isinstance(p, int) and p < 2):
                    load(p, b)
                p, b = pair(t, k, "l3b")
                if p is not None:
                    passed(sp, "x4_done", p)
                    sp.dma_start(out_pairs[bass.ds(index(p), 1)].rearrange("o n g d -> (o n) g d"), x4[:, b]).then_inc(x_out[b], 16)

            load(0, 0)
            load(1, 1)
            for dst, src in ((w0_sb[:], w0t.rearrange("(c p) o -> p c o", p=P)),
                             (deg_b[:], bias0.partition_broadcast(P)),
                             (w1_sb[:, :, 0:D], w1.rearrange("(c p) o -> p c o", p=P)),
                             (w1t_sb[:], w1t.rearrange("(c p) o -> p c o", p=P)),
                             (a1_sb[:], a1.rearrange("(c p) o -> p c o", p=P)),
                             (w2_sb[:, :, 0:F1], w2.rearrange("(c p) o -> p c o", p=P)),
                             (w2t_sb[:], w2t), (a2_sb[:], a2),
                             (wq_sb[:], wqt.rearrange("(c p) o -> p c o", p=P)),
                             (wk_sb[:], wkt.rearrange("(c p) o -> p c o", p=P)),
                             (wv_sb[:], wvt.rearrange("(c p) o -> p c o", p=P)),
                             (wo_sb[:], wot.rearrange("(c p) o -> p c o", p=P)),
                             (bq_sb[:], bq), (bk_sb[:], bk), (bv_sb[:], bv),
                             (c3[:], bo.partition_broadcast(P))):
                sp.dma_start(dst, src).then_inc(weights_in, 16)

            run_steps(sp, step)
            sp.wait_ge(x_out[0], 16 * (NP // 2))
            sp.wait_ge(x_out[1], 16 * (NP // 2))

        n_weights = 16

        @block.gpsimd
        def _(pool):
            pool.memset(power[:], -0.5).then_inc(c_pool, 1)
            pool.memset(eps[:], LN_EPS)
            pool.memset(minus_one[:], -1.0)
            pool.memset(ident[:], 0.0).then_inc(c_pool, 1)
            pool.wait_ge(c_pool, 2)
            pool.affine_select(out=ident[:], in_=ident[:], compare_op=ALU.not_equal, fill=1.0, base=0,
                               pattern=[[-1, P]], channel_multiplier=1).then_inc(c_pool, 1)
            pool.wait_ge(c_dve, 10)

            def norm_scale(i, p, b):
                passed(pool, f"mv{i}", p)
                passed(pool, "h0_hi" if i == 0 else f"y{i}", p, 2)
                pool.tensor_tensor(veps[i][:, b], mv[i][:, b, :, 1], eps[:], ALU.add).then_inc(S[f"veps{i}"], 1)
                passed(pool, f"veps{i}", p)
                pool.tensor_tensor(rstd[i][:, b], veps[i][:, b], power[:], ALU.pow).then_inc(S[f"rstd{i}"], 1)

            def normalise_p3(j, p, b):
                passed(pool, f"rsum3_{j}", p)
                passed(pool, f"exp3_{j}", p)
                passed(pool, f"pt{j}_full", p, 1)
                pool.tensor_tensor(probs3[:, j], exps3_sb[:, j], rsum3[:, b, j].unsqueeze(2).to_broadcast([P, DC * G, P]),
                                   ALU.mult).then_inc(S[f"p3_{j}"], 1)

            def step(t, k):
                pp, bp = pair(t, k, "pre")
                p0, b0 = pair(t, k, "l0")
                p2, b2 = pair(t, k, "l2")
                p3, b3 = pair(t, k, "l3")
                p4, b4 = pair(t, k, "l3b")
                if p4 is not None:
                    normalise_p3(2, p4, b4)
                if p3 is not None:
                    passed(pool, "hh_done", p3)
                    passed(pool, "y3", p3, 2)
                    passed(pool, "r3", p3, 2)
                    pool.tensor_tensor(x3[:, b3, :, F1:D], x2[:, b3, :, F1:D], hh[:, b3, :, 0:F1],
                                       ALU.add).then_inc(S["x3_tail"], 1)
                if p4 is not None:
                    normalise_p3(0, p4, b4)
                    normalise_p3(3, p4, b4)
                    normalise_p3(1, p4, b4)
                if p2 is not None:
                    norm_scale(2, p2, b2)
                if p3 is not None:
                    norm_scale(3, p3, b3)
                if p0 is not None:
                    pool.wait_ge(x_in[b0], dma_count(p0, b0))
                    passed(pool, "x1_done", p0, 2)
                    pool.tensor_tensor(r0[:, b0], x0[:, b0], deg_b[:].unsqueeze(1).to_broadcast([P, G, D]),
                                       ALU.add).then_inc(S["r0"], 1)
                if p3 is not None:
                    passed(pool, "x4_done", p3, 2)
                    passed(pool, "x3_done", p3)
                    pool.tensor_tensor(r3[:, b3], x3[:, b3], c3[:].unsqueeze(1).to_broadcast([P, G, D]),
                                       ALU.add).then_inc(S["r3"], 1)
                if pp is not None:
                    norm_scale(0, pp, bp)
                    passed(pool, "h0_hi", pp, 2)
                    pool.tensor_tensor(negmean[:, bp], mv[0][:, bp, :, 0], minus_one[:], ALU.mult).then_inc(S["negmean"], 1)
                    passed(pool, "negmean", pp)
                    passed(pool, "rstd0", pp)
                    pool.tensor_tensor(nmr[:, bp], negmean[:, bp], rstd[0][:, bp], ALU.mult).then_inc(S["nmr"], 1)
                    passed(pool, "h0_hi", pp)
                    passed(pool, "h0", pp)
                    passed(pool, "u1_full", pp, 2)
                    pool.tensor_tensor(h0_r[1][:, bp], h0[:, bp], h0_r[0][:, bp].bitcast(F32), ALU.subtract).then_inc(S["h0_lo"], 1)
                if p0 is not None:
                    norm_scale(1, p0, b0)

            run_steps(pool, step)

        @block.vector
        def _(dve):
            dve.wait_ge(adj_in, 16)
            dve.tensor_copy(adj_f[:], adj_i[:]).then_inc(c_dve, 1)
            dve.wait_ge(c_dve, 1)
            dve.reduce_sum(deg[:], adj_f[:], AX.X).then_inc(c_dve, 1)
            dve.tensor_scalar(mask[:], adj_f[:], 0.0, MASKED, ALU.is_equal, ALU.mult).then_inc(c_dve, 1)
            dve.tensor_scalar(mask2[:], adj_f[:], 1.0, NEG, ALU.subtract, ALU.mult)
            dve.wait_ge(c_dve, 3)
            dve.wait_ge(c_pool, 3)
            dve.tensor_copy(mask_bf[:], mask[:])
            dve.tensor_copy(ident_bf[:], ident[:])
            dve.tensor_scalar(aggr_r[:, P:2 * P], ident[:], deg[:], None, ALU.mult)
            dve.wait_ge(weights_in, 16 * n_weights)
            dve.tensor_scalar(deg_b[:], deg_b[:], deg[:], None, ALU.mult)
            dve.reduce_max(has_any[:], mask[:], AX.X).then_inc(c_dve, 1)
            dve.wait_ge(c_dve, 4)
            dve.tensor_scalar(has_any[:], has_any[:], 0.0, None, ALU.is_equal).then_inc(c_dve, 1)
            dve.wait_ge(c_dve, 5)
            dve.reciprocal(nan_row[:], has_any[:]).then_inc(c_dve, 1)
            dve.wait_ge(c_dve, 6)
            dve.tensor_scalar(nan_row[:], nan_row[:], 0.0, None, ALU.mult).then_inc(c_dve, 1)
            for w, (hi, lo) in ((w0_sb, w0_r), (wq_sb, wq_r), (wk_sb, wk_r), (wv_sb, wv_r), (wo_sb, wo_r)):
                last = dve.tensor_copy(hi[:], w[:])
            last.then_inc(c_split, 1)
            dve.wait_ge(c_split, 1)
            for w, (hi, lo) in ((w0_sb, w0_r), (wq_sb, wq_r), (wk_sb, wk_r), (wv_sb, wv_r), (wo_sb, wo_r)):
                dve.tensor_tensor(lo[:], w[:], hi[:].bitcast(F32), ALU.subtract)
            dve.wait_ge(c_pe, 1)
            dve.wait_ge(c_dve, 7)
            dve.tensor_copy(aggr_r[:, 0:P], general_bank[0][:, 0:P])
            for c in range(DC):
                dve.tensor_copy(w1_sb[:, c, D:D + 2], general_bank[1][:, 2 * c:2 * c + 2])
                dve.tensor_copy(w2_sb[:, c, F1:F1 + 2], general_bank[2][:, 2 * c:2 * c + 2])
            dve.scalar_tensor_tensor(c3[:], general_bank[3][:, 0:D], nan_row[:], c3[:], ALU.add, ALU.add).then_inc(c_dve, 1)
            dve.wait_ge(c_dve, 8)
            dve.tensor_copy(w1_r[0][:], w1_sb[:]).then_inc(c_dve, 1)
            dve.wait_ge(c_dve, 9)
            dve.tensor_tensor(w1_r[1][:], w1_sb[:], w1_r[0][:].bitcast(F32), ALU.subtract).then_inc(c_dve, 1)

            def norm_stats(i, src, p, b):
                passed(dve, f"rstd{i}", p, 2)
                if i == 0:
                    passed(dve, "negmean", p, 2)
                passed(dve, "h0_hi" if i == 0 else f"y{i}", p, 2)
                for g in range(G):
                    last = dve.bn_stats(stats[i][:, b, g], src[:, b, g])
                last.then_inc(S[f"stats{i}"], 1)
                dve.wait_ge(c_dve, 10)
                passed(dve, f"stats{i}", p)
                for g in range(G):
                    last = dve.bn_aggr(mv[i][:, b, g], stats[i][:, b, g])
                last.then_inc(S[f"mv{i}"], 1)

            def normalise(i, src, p, b):
                passed(dve, f"rstd{i}", p)
                passed(dve, f"mv{i}", p)
                passed(dve, f"h{i}t_full", p, 2)
                for g in range(G):
                    last = dve.tensor_scalar(y[i][:, b, g], src[:, b, g], mv[i][:, b, g, 0:1], rstd[i][:, b, g:g + 1],
                                             ALU.subtract, ALU.mult)
                last.then_inc(S[f"y{i}"], 1)

            def logits(i, msk, p, b):
                passed(dve, f"d{i}_done", p)
                dve.scalar_tensor_tensor(z[i][:, b], z[i][:, b], SLOPE, z[i][:, b], ALU.mult, ALU.max).then_inc(S[f"leaky{i}"], 1)
                passed(dve, f"leaky{i}", p)
                dve.tensor_tensor(z[i][:, b], z[i][:, b], msk[:].unsqueeze(1).to_broadcast([P, G, P]), ALU.add).then_inc(S[f"logit{i}"], 1)
                passed(dve, f"logit{i}", p)
                dve.tensor_reduce(nmax[i][:, b], z[i][:, b], AX.X, ALU.max, negate=True).then_inc(S[f"nmax{i}"], 1)

            def reciprocal3(j, p, b):
                passed(dve, f"exp3_{j}", p)
                passed(dve, f"p3_{j}", p, 2)
                dve.reciprocal(rsum3[:, b, j], ssum3[:, b, j]).then_inc(S[f"rsum3_{j}"], 1)

            def scores(j, p, b):
                passed(dve, "scores_full", p)
                passed(dve, f"exp3_{j}", p, 2)
                dve.tensor_reduce(nmax3[:, b, j], score_bank[j][:].rearrange("p (b n) -> p b n", n=P), AX.X, ALU.max,
                                  negate=True).then_inc(S[f"nmax3_{j}"], 1)

            def relu_transposed_low(i, dst, reader, p, b):
                passed(dve, f"h{i}t_hi", p)
                passed(dve, reader, p, 2)
                dve.scalar_tensor_tensor(dst[1][:, b].rearrange("p c g n -> p (c g n)"), bank_of(f"h{i}t_done")[:], 0.0,
                                         dst[0][:, b].rearrange("p c g n -> p (c g n)").bitcast(F32),
                                         ALU.max, ALU.subtract).then_inc(S[f"h{i}t_done"], 1)

            def low_u(g, p, b):
                passed(dve, f"u{g}_hi", p)
                passed(dve, "x1_full", p, 2)
                dve.tensor_tensor(ut_r[1][:, b, g].rearrange("p c n -> p (c n)"), bank_of(f"u{g}_done")[:],
                                  ut_r[0][:, b, g].rearrange("p c n -> p (c n)").bitcast(F32), ALU.subtract).then_inc(S[f"u{g}_done"], 1)

            def add_bias(name, dst, bias, scale, p, b):
                passed(dve, f"{name}_full", p)
                passed(dve, "scores_full", p, 2)
                for c in range(DC):
                    last = dve.tensor_scalar(dst[:, b, c], bank_of(f"{name}_done")[:, c * G * P:(c + 1) * G * P], bias[:, c:c + 1], scale,
                                             ALU.add, ALU.mult)
                last.then_inc(S[f"{name}_done"], 1)

            def step(t, k):
                pp, bp = pair(t, k, "pre")
                p0, b0 = pair(t, k, "l0")
                p1, b1 = pair(t, k, "l1")
                p2, b2 = pair(t, k, "l2")
                p3, b3 = pair(t, k, "l3")
                p4, b4 = pair(t, k, "l3b")
                if p2 is not None:
                    normalise(2, x2, p2, b2)
                if p3 is not None:
                    normalise(3, x3, p3, b3)
                if p4 is not None:
                    passed(dve, "ot_hi", p4)
                    passed(dve, "x4_full", p4, 2)
                    dve.tensor_tensor(ot_r[1][:, b4].rearrange("p c n -> p (c n)"), bank_of("ot_done")[:],
                                      ot_r[0][:, b4].rearrange("p c n -> p (c n)").bitcast(F32), ALU.subtract).then_inc(S["ot_done"], 1)
                if p3 is not None:
                    relu_transposed_low(3, ht3_r, "v_full", p3, b3)
                if pp is not None:
                    dve.wait_ge(x_in[bp], dma_count(pp, bp))
                    norm_stats(0, x0, pp, bp)
                if p1 is not None:
                    logits(1, mask, p1, b1)
                if p3 is not None:
                    add_bias("kt", kt, bk_sb, 1.0, p3, b3)
                    add_bias("qt", qt, bq_sb, float(DH) ** -0.5, p3, b3)
                if p2 is not None:
                    logits(2, mask2, p2, b2)
                if p3 is not None:
                    scores(2, p3, b3)
                    scores(0, p3, b3)
                    scores(3, p3, b3)
                if p1 is not None:
                    passed(dve, "exp1", p1)
                    passed(dve, "x2_done", p1, 2)
                    dve.reciprocal(rsum[1][:, b1], ssum[1][:, b1]).then_inc(S["rsum1_any"], 1)
                    passed(dve, "rsum1_any", p1)
                    dve.tensor_scalar(rsum[1][:, b1], rsum[1][:, b1], has_any[:], None, ALU.mult).then_inc(S["rsum1"], 1)
                if p3 is not None:
                    scores(1, p3, b3)
                    reciprocal3(2, p3, b3)
                if p0 is not None:
                    passed(dve, "x1_full", p0)
                    passed(dve, "r0", p0)
                    passed(dve, "x2_done", p0, 2)
                    passed(dve, "y1", p0, 2)
                    dve.tensor_tensor(x1[:, b0].rearrange("p g d -> p (g d)"), bank_of("x1_done")[:],
                                      r0[:, b0].rearrange("p g d -> p (g d)"), ALU.add).then_inc(S["x1_done"], 1)
                    passed(dve, "x1_done", p0)
                    norm_stats(1, x1, p0, b0)
                if p1 is not None:
                    passed(dve, "x2_full", p1)
                    passed(dve, "rsum1", p1)
                    passed(dve, "x3_done", p1, 2)
                    passed(dve, "x3_tail", p1, 2)
                    passed(dve, "y2", p1, 2)
                    for g in range(G):
                        last = dve.scalar_tensor_tensor(x2[:, b1, g], bank_of("x2_done")[:, g * D:(g + 1) * D], rsum[1][:, b1, g:g + 1],
                                                        x1[:, b1, g], ALU.mult, ALU.add)
                    last.then_inc(S["x2_done"], 1)
                if p3 is not None:
                    reciprocal3(0, p3, b3)
                if p2 is not None:
                    passed(dve, "exp2", p2)
                    passed(dve, "x3_done", p2, 2)
                    dve.reciprocal(rsum[2][:, b2], ssum[2][:, b2]).then_inc(S["rsum2"], 1)
                if p0 is not None:
                    normalise(1, x1, p0, b0)
                if pp is not None:
                    low_u(1, pp, bp)
                if p4 is not None:
                    passed(dve, "x4_full", p4)
                    passed(dve, "r3", p4)
                    if not isinstance(p4, int) or p4 >= 2:
                        dve.wait_ge(x_out[b4], dma_count(p4, b4, 2))
                    dve.tensor_tensor(x4[:, b4].rearrange("p g d -> p (g d)"), bank_of("x4_done")[:],
                                      r3[:, b4].rearrange("p g d -> p (g d)"), ALU.add).then_inc(S["x4_done"], 1)
                if p3 is not None:
                    reciprocal3(3, p3, b3)
                    reciprocal3(1, p3, b3)
                if p0 is not None:
                    relu_transposed_low(1, ht1_r, "wh1_full", p0, b0)
                if pp is not None:
                    low_u(0, pp, bp)
                if p2 is not None:
                    passed(dve, "x3_full", p2)
                    passed(dve, "rsum2", p2)
                    passed(dve, "y3", p2, 2)
                    passed(dve, "r3", p2, 2)
                    for g in range(G):
                        last = dve.scalar_tensor_tensor(x3[:, b2, g, 0:F1], bank_of("x3_done")[:, g * F1:(g + 1) * F1], rsum[2][:, b2, g:g + 1],
                                                        x2[:, b2, g, 0:F1], ALU.mult, ALU.add)
                    last.then_inc(S["x3_done"], 1)
                if p1 is not None:
                    passed(dve, "x2_done", p1)
                    norm_stats(2, x2, p1, b1)
                if p2 is not None:
                    passed(dve, "x3_done", p2)
                    passed(dve, "x3_tail", p2)
                    norm_stats(3, x3, p2, b2)

            run_steps(dve, step)

        @block.scalar
        def _(act):
            act.wait_ge(weights_in, 16 * n_weights)

            def exps(i, p, b):
                passed(act, f"nmax{i}", p)
                passed(act, f"at{i}_full", p, 2)
                passed(act, f"rsum{i}", p, 2)
                for g in range(G):
                    last = act.activation(ez[i][:, b, g], z[i][:, b, g], ACT.Exp, bias=nmax[i][:, b, g:g + 1],
                                          accum_out=ssum[i][:, b, g:g + 1])
                last.then_inc(S[f"exp{i}"], 1)

            def sum_logits(i, src, scol, p, b):
                passed(act, f"d{i}_full", p)
                passed(act, f"exp{i}", p, 2)
                bank = bank_of(f"d{i}_done")
                for g in range(G):
                    last = act.activation(z[i][:, b, g], bank[:, g * P:(g + 1) * P], ACT.Identity, bias=src[:, b, g, scol:scol + 1])
                last.then_inc(S[f"d{i}_done"], 1)

            def relu_transposed_high(i, dst, reader, p, b):
                passed(act, f"h{i}t_full", p)
                passed(act, reader, p, 2)
                passed(act, f"h{i}t_done", p, 2)
                act.activation(dst[0][:, b].rearrange("p c g n -> p (c g n)"), bank_of(f"h{i}t_done")[:], ACT.Relu).then_inc(S[f"h{i}t_hi"], 1)

            def copy_p3_transposed(j, p):
                passed(act, f"pt{j}_full", p)
                passed(act, "ot_full", p, 1)
                act.activation(probs3_t[:, j].rearrange("p b n -> p (b n)"), bank_of(f"pt{j}_done")[:], ACT.Copy).then_inc(S[f"pt{j}_done"], 1)

            def exp_transposed(i, p, b):
                passed(act, f"at{i}_full", p)
                passed(act, f"x{i + 1}_full", p, 2)
                act.activation(at[i][:, b].rearrange("p g n -> p (g n)"), bank_of(f"at{i}_done")[:, 0:G * P], ACT.Copy).then_inc(S[f"at{i}_done"], 1)

            def copy_projection1(g, p, b):
                passed(act, f"wh{g}_full", p)
                passed(act, "x2_full", p, 2)
                passed(act, "d1_done", p, 2)
                act.activation(wh[:, b, g], bank_of(f"wh{g}_done")[:, 0:D + 2], ACT.Copy).then_inc(S[f"wh{g}_done"], 1)

            def high_u(g, p, b):
                passed(act, f"u{g}_full", p)
                passed(act, "x1_full", p, 2)
                passed(act, f"u{g}_done", p, 2)
                act.activation(ut_r[0][:, b, g].rearrange("p c n -> p (c n)"), bank_of(f"u{g}_done")[:], ACT.Copy).then_inc(S[f"u{g}_hi"], 1)

            def exps3(j, p, b):
                passed(act, f"nmax3_{j}", p)
                passed(act, f"p3_{j}", p, 1)
                passed(act, f"rsum3_{j}", p, 2)
                for i in range(DC * G):
                    last = act.activation(exps3_sb[:, j, i], score_bank[j][:, i * P:(i + 1) * P], ACT.Exp, bias=nmax3[:, b, j, i:i + 1],
                                          accum_out=ssum3[:, b, j, i:i + 1])
                last.then_inc(S[f"exp3_{j}"], 1)

            def step(t, k):
                pp, bp = pair(t, k, "pre")
                p0, b0 = pair(t, k, "l0")
                p1, b1 = pair(t, k, "l1")
                p2, b2 = pair(t, k, "l2")
                p3, b3 = pair(t, k, "l3")
                p4, b4 = pair(t, k, "l3b")
                if p0 is not None:
                    high_u(0, p0, b0)
                if p4 is not None:
                    copy_p3_transposed(0, p4)
                    copy_p3_transposed(2, p4)
                    copy_p3_transposed(3, p4)
                    copy_p3_transposed(1, p4)
                if p1 is not None:
                    copy_projection1(1, p1, b1)
                    copy_projection1(0, p1, b1)
                if p4 is not None:
                    passed(act, "ot_full", p4)
                    passed(act, "x4_full", p4, 2)
                    passed(act, "ot_done", p4, 2)
                    act.activation(ot_r[0][:, b4].rearrange("p c n -> p (c n)"), bank_of("ot_done")[:], ACT.Copy).then_inc(S["ot_hi"], 1)
                if p2 is not None:
                    passed(act, "h2t_full", p2)
                    passed(act, "hh_full", p2, 2)
                    act.activation(ht2[:, b2].rearrange("p c g n -> p (c g n)"), bank_of("h2t_done")[:], ACT.Relu).then_inc(S["h2t_done"], 1)
                if p3 is not None:
                    relu_transposed_high(3, ht3_r, "v_full", p3, b3)
                if p1 is not None:
                    sum_logits(1, wh, D, p1, b1)
                if p2 is not None:
                    passed(act, "hh_full", p2)
                    passed(act, "x3_full", p2, 2)
                    passed(act, "d2_done", p2, 2)
                    passed(act, "x3_tail", p2, 2)
                    act.activation(hh[:, b2].rearrange("p g n -> p (g n)"), bank_of("hh_done")[:, 0:G * (F1 + 2)], ACT.Copy).then_inc(S["hh_done"], 1)
                if p1 is not None:
                    exps(1, p1, b1)
                if p2 is not None:
                    sum_logits(2, hh, F1, p2, b2)
                if p1 is not None:
                    exp_transposed(1, p1, b1)
                if pp is not None:
                    passed(act, "u1_full", pp, 2)
                    passed(act, "h0_lo", pp, 2)
                    passed(act, "nmr", pp)
                    for g in range(G):
                        last = act.activation(h0_r[0][:, bp, g], x0[:, bp, g], ACT.Relu, bias=nmr[:, bp, g:g + 1], scale=rstd[0][:, bp, g:g + 1])
                    last.then_inc(S["h0_hi"], 1)
                if p2 is not None:
                    exps(2, p2, b2)
                if pp is not None:
                    passed(act, "u1_full", pp, 2)
                    passed(act, "h0_lo", pp, 2)
                    passed(act, "nmr", pp)
                    for g in range(G):
                        last = act.activation(h0[:, bp, g], x0[:, bp, g], ACT.Relu, bias=nmr[:, bp, g:g + 1], scale=rstd[0][:, bp, g:g + 1])
                    last.then_inc(S["h0"], 1)
                if p3 is not None:
                    exps3(2, p3, b3)
                    exps3(0, p3, b3)
                if p2 is not None:
                    exp_transposed(2, p2, b2)
                if p3 is not None:
                    exps3(3, p3, b3)
                    passed(act, "v_full", p3)
                    passed(act, "ot_full", p3, 2)
                    act.activation(v[:, b3].rearrange("p g d -> p (g d)"), bank_of("v_done")[:], ACT.Copy).then_inc(S["v_done"], 1)
                if pp is not None:
                    high_u(1, pp, bp)
                if p3 is not None:
                    exps3(1, p3, b3)
                if p0 is not None:
                    relu_transposed_high(1, ht1_r, "wh1_full", p0, b0)

            run_steps(act, step)

        @block.tensor
        def _(pe):
            pe.wait_ge(c_pool, 3)
            pe.wait_ge(c_dve, 1)
            pe.wait_ge(weights_in, 16 * n_weights)
            pe.transpose(general_bank[0][:, 0:P], adj_f[:], ident[:])
            for c in range(DC):
                for e in range(DC):
                    pe.matmul(general_bank[1][:, 2 * c:2 * c + 2], w1t_sb[:, e, c * P:(c + 1) * P], a1_sb[:, e, :],
                              start=(e == 0), stop=(e == DC - 1))
                pe.matmul(general_bank[2][:, 2 * c:2 * c + 2], w2t_sb[:, c * P:(c + 1) * P], a2_sb[:], start=True, stop=True)
            for c in range(DC):
                last = pe.matmul(general_bank[3][:, 0:D], bv_sb[:, c:c + 1].to_broadcast([P, P]), wo_sb[:, c, :],
                                 start=(c == 0), stop=(c == DC - 1))
            last.then_inc(c_pe, 1)
            pe.wait_ge(c_dve, 10)

            def split_matmul(out_ap, lhs, rhs, start, stop):
                pe.matmul(out_ap, lhs[0], rhs[0], start=start, stop=False)
                pe.matmul(out_ap, lhs[0], rhs[1], start=False, stop=False)
                return pe.matmul(out_ap, lhs[1], rhs[0], start=False, stop=stop)

            def transpose_y(i, p, b, t, k):
                passed(pe, f"y{i}", p)
                bank_free(pe, f"h{i}t_done", t, k)
                for c in range(DC):
                    for g in range(G):
                        last = pe.transpose(bank_of(f"h{i}t_done")[:, (c * G + g) * P:(c * G + g + 1) * P], y[i][:, b, g, c * P:(c + 1) * P], ident[:])
                last.then_inc(S[f"h{i}t_full"], 1)

            def spread_dst(i, src, col, p, b, t, k):
                bank_free(pe, f"d{i}_done", t, k)
                for g in range(G):
                    last = pe.transpose(bank_of(f"d{i}_done")[:, g * P:(g + 1) * P], src[:, b, g, col:col + 1].to_broadcast([P, P]), ident[:])
                last.then_inc(S[f"d{i}_full"], 1)

            def transpose_exp(i, p, b, t, k):
                passed(pe, f"exp{i}", p)
                bank_free(pe, f"at{i}_done", t, k)
                for g in range(G):
                    last = pe.transpose(bank_of(f"at{i}_done")[:, g * P:(g + 1) * P], ez[i][:, b, g], ident[:])
                last.then_inc(S[f"at{i}_full"], 1)

            def project1(g, p, b, t, k):
                passed(pe, "h1t_done", p)
                bank_free(pe, f"wh{g}_done", t, k)
                for c in range(DC):
                    last = split_matmul(bank_of(f"wh{g}_done")[:, 0:D + 2], [h_[:, b, c, g] for h_ in ht1_r], [w_[:, c, :] for w_ in w1_r],
                                        c == 0, c == DC - 1)
                last.then_inc(S[f"wh{g}_full"], 1)

            def scores(c, p, b):
                passed(pe, "qt_done", p)
                passed(pe, "kt_done", p)
                for g in range(G):
                    for j in range(HPC):
                        r = slice(j * DH, (j + 1) * DH)
                        last = pe.matmul(score_bank[j][:, (c * G + g) * P:(c * G + g + 1) * P], qt[r, b, c, g * P:(g + 1) * P],
                                         kt[r, b, c, g * P:(g + 1) * P], start=False, stop=(c == DC - 1 and g == G - 1), tile_position=(j * DH, 0))
                return last

            def start_scores(j, p):
                passed(pe, f"exp3_{j}", p, 1)
                pe.matmul(score_bank[j][:], ident_bf[:], mask_bf[:].unsqueeze(1).to_broadcast([P, DC * G, P]), start=True, stop=False)

            def aggregate(g, p, b, t, k):
                passed(pe, "h0_hi", p)
                passed(pe, "h0_lo", p)
                bank_free(pe, f"u{g}_done", t, k)
                for c in range(DC):
                    for part in range(2):
                        last = pe.matmul(bank_of(f"u{g}_done")[:, c * 2 * P:(c + 1) * 2 * P], h0_r[part][:, b, g, c * P:(c + 1) * P], aggr_r[:],
                                         start=(part == 0), stop=(part == 1))
                last.then_inc(S[f"u{g}_full"], 1)

            def transpose_p3(j, p, b, t, k):
                passed(pe, f"p3_{j}", p)
                bank_free(pe, f"pt{j}_done", t, k)
                for i in range(DC * G):
                    last = pe.transpose(bank_of(f"pt{j}_done")[:, i * P:(i + 1) * P], probs3[:, j, i], ident[:])
                last.then_inc(S[f"pt{j}_full"], 1)

            def step(t, k):
                pp, bp = pair(t, k, "pre")
                p0, b0 = pair(t, k, "l0")
                p1, b1 = pair(t, k, "l1")
                p2, b2 = pair(t, k, "l2")
                p3, b3 = pair(t, k, "l3")
                p4, b4 = pair(t, k, "l3b")
                if p3 is not None:
                    passed(pe, "at2_done", p3)
                    bank_free(pe, "x3_done", t, k)
                    for g in range(G):
                        last = pe.matmul(bank_of("x3_done")[:, g * F1:(g + 1) * F1], at[2][:, b3, g], hh[:, b3, g, 0:F1], start=True, stop=True)
                    last.then_inc(S["x3_full"], 1)
                if p4 is not None:
                    transpose_p3(0, p4, b4, t, k)
                    transpose_p3(2, p4, b4, t, k)
                    transpose_p3(3, p4, b4, t, k)
                if p1 is not None:
                    project1(1, p1, b1, t, k)
                if p4 is not None:
                    transpose_p3(1, p4, b4, t, k)
                if p1 is not None:
                    project1(0, p1, b1, t, k)
                if p4 is not None:
                    for j in range(HPC):
                        passed(pe, f"pt{j}_done", p4)
                    passed(pe, "v_done", p4)
                    bank_free(pe, "ot_done", t, k)
                    for c in range(DC):
                        for g in range(G):
                            for j in range(HPC):
                                last = pe.matmul(bank_of("ot_done")[j * DH:(j + 1) * DH, (c * G + g) * P:(c * G + g + 1) * P],
                                                 v[:, b4, g, c * P + j * DH:c * P + (j + 1) * DH], probs3_t[:, j, c * G + g], start=True, stop=True, tile_position=(0, j * DH))
                    last.then_inc(S["ot_full"], 1)
                if p2 is not None:
                    transpose_y(2, p2, b2, t, k)
                if p3 is not None:
                    transpose_y(3, p3, b3, t, k)
                if p1 is not None:
                    passed(pe, "wh0_done", p1)
                    passed(pe, "wh1_done", p1)
                    spread_dst(1, wh, D + 1, p1, b1, t, k)
                if p2 is not None:
                    passed(pe, "h2t_done", p2)
                    bank_free(pe, "hh_done", t, k)
                    for g in range(G):
                        for c in range(DC):
                            last = pe.matmul(bank_of("hh_done")[:, g * (F1 + 2):(g + 1) * (F1 + 2)], ht2[:, b2, c, g], w2_sb[:, c, :], start=(c == 0), stop=(c == DC - 1))
                    last.then_inc(S["hh_full"], 1)
                if p3 is not None:
                    passed(pe, "h3t_done", p3)
                    bank_free(pe, "kt_done", t, k)
                    for o in range(DC):
                        for c in range(DC):
                            last = split_matmul(bank_of("kt_done")[:, o * G * P:(o + 1) * G * P], [w_[:, c, o * P:(o + 1) * P] for w_ in wk_r],
                                                [h_[:, b3, c].rearrange("p g n -> p (g n)") for h_ in ht3_r], c == 0, c == DC - 1)
                    last.then_inc(S["kt_full"], 1)
                    passed(pe, "h3t_done", p3)
                    bank_free(pe, "qt_done", t, k)
                    for o in range(DC):
                        for c in range(DC):
                            last = split_matmul(bank_of("qt_done")[:, o * G * P:(o + 1) * G * P], [w_[:, c, o * P:(o + 1) * P] for w_ in wq_r],
                                                [h_[:, b3, c].rearrange("p g n -> p (g n)") for h_ in ht3_r], c == 0, c == DC - 1)
                    last.then_inc(S["qt_full"], 1)
                if p2 is not None:
                    passed(pe, "hh_done", p2)
                    spread_dst(2, hh, F1 + 1, p2, b2, t, k)
                if p3 is not None:
                    start_scores(3, p3)
                if p1 is not None:
                    transpose_exp(1, p1, b1, t, k)
                if p3 is not None:
                    start_scores(2, p3)
                    start_scores(1, p3)
                    scores(0, p3, b3)
                    scores(1, p3, b3).then_inc(S["scores_full"], 1)
                if p0 is not None:
                    passed(pe, "u0_done", p0)
                    passed(pe, "u1_done", p0)
                    bank_free(pe, "x1_done", t, k)
                    for g in range(G):
                        for c in range(DC):
                            for side in range(2):
                                last = split_matmul(bank_of("x1_done")[:, g * D:(g + 1) * D], [u_[:, b0, g, c, side * P:(side + 1) * P] for u_ in ut_r],
                                                    [w[:, (1 - side) * DC + c, :] for w in w0_r], c == 0 and side == 0, c == DC - 1 and side == 1)
                    last.then_inc(S["x1_full"], 1)
                if p2 is not None:
                    transpose_exp(2, p2, b2, t, k)
                if p3 is not None:
                    passed(pe, "h3t_done", p3)
                    bank_free(pe, "v_done", t, k)
                    for g in range(G):
                        for c in range(DC):
                            last = split_matmul(bank_of("v_done")[:, g * D:(g + 1) * D], [h_[:, b3, c, g] for h_ in ht3_r],
                                                [w_[:, c, :] for w_ in wv_r], c == 0, c == DC - 1)
                    last.then_inc(S["v_full"], 1)
                if p1 is not None:
                    passed(pe, "at1_done", p1)
                    bank_free(pe, "x2_done", t, k)
                    for g in range(G):
                        last = pe.matmul(bank_of("x2_done")[:, g * D:(g + 1) * D], at[1][:, b1, g], wh[:, b1, g, 0:D], start=True, stop=True)
                    last.then_inc(S["x2_full"], 1)
                if pp is not None:
                    aggregate(1, pp, bp, t, k)
                if p4 is not None:
                    passed(pe, "ot_done", p4)
                    bank_free(pe, "x4_done", t, k)
                    for g in range(G):
                        for c in range(DC):
                            last = split_matmul(bank_of("x4_done")[:, g * D:(g + 1) * D], [o_[:, b4, c, g * P:(g + 1) * P] for o_ in ot_r],
                                                [w_[:, c, :] for w_ in wo_r], c == 0, c == DC - 1)
                    last.then_inc(S["x4_full"], 1)
                if p0 is not None:
                    transpose_y(1, p0, b0, t, k)
                if p2 is not None:
                    start_scores(0, p2)
                if pp is not None:
                    aggregate(0, pp, bp, t, k)

            run_steps(pe, step)


def kernel(x, adj, L0_gnn_W, L0_gnn_b, L1_gnn_W, L1_gnn_a_src, L1_gnn_a_dst, L2_gnn_W, L2_gnn_a, L3_gnn_Wq, L3_gnn_bq,
           L3_gnn_Wk, L3_gnn_bk, L3_gnn_Wv, L3_gnn_bv, L3_gnn_Wo, L3_gnn_bo):
    import numpy as np
    import concourse.bacc as bacc
    from concourse.bass_utils import run_bass_kernel_spmd

    def columns(b):
        return np.asarray(b).reshape(DC, P).T

    ins = {
        "x": x, "adj": adj, "w0t": np.asarray(L0_gnn_W).T, "b0": L0_gnn_b,
        "w1": L1_gnn_W, "w1t": np.asarray(L1_gnn_W).T,
        "a1": np.stack([np.asarray(L1_gnn_a_src), np.asarray(L1_gnn_a_dst)], axis=1),
        "w2": L2_gnn_W, "w2t": np.asarray(L2_gnn_W).T, "a2": np.asarray(L2_gnn_a)[:, :, 0].T,
        "wqt": np.asarray(L3_gnn_Wq).T, "bq": columns(L3_gnn_bq),
        "wkt": np.asarray(L3_gnn_Wk).T, "bk": columns(L3_gnn_bk),
        "wvt": np.asarray(L3_gnn_Wv).T, "bv": columns(L3_gnn_bv),
        "wot": np.asarray(L3_gnn_Wo).T, "bo": L3_gnn_bo,
    }
    nc = bacc.Bacc("TRN2", target_bir_lowering=False, num_devices=1)
    arrays, args = {}, []
    for name, a in ins.items():
        arrays[f"in_{name}"] = a = np.ascontiguousarray(a)
        args.append(nc.dram_tensor(f"in_{name}", a.shape, mybir.dt.from_np(a.dtype), kind="ExternalInput").ap())
    args.append(nc.dram_tensor("out", arrays["in_x"].shape, F32, kind="ExternalOutput").ap())
    gnn_kernel(nc, *args)
    r = run_bass_kernel_spmd(nc, [arrays], core_ids=[0])
    return r.results[0]["out"]
```
